# Optimizing a Trainium2 kernel written in Bass

```python
import numpy as np
import jax
import jax.numpy as jnp

def _softmax(x, axis=-1):
    return jax.nn.softmax(x, axis=axis)

def _gelu(x):
    return jax.nn.gelu(x, approximate=True)

def _silu(x):
    return jax.nn.silu(x)

def _sigmoid(x):
    return jax.nn.sigmoid(x)

def _layernorm(x, axis=-1, eps=1e-05):
    m = jnp.mean(x, axis=axis, keepdims=True)
    v = jnp.var(x, axis=axis, keepdims=True)
    return (x - m) / jnp.sqrt(v + eps)

def _scatter_add(tgt, idx, src, axis=0):
    return tgt.at[idx].add(src)

def _segment_sum(src, seg, n):
    return jax.ops.segment_sum(src, seg, n)
kernel_name = 'mk_prb_d1_jaxref_r8_938b06'

def setup_inputs(seed: int=0):
    np.random.seed(seed)
    _w = jnp.asarray

    def _L0_attn_setup():
        import jax, jax.numpy as jnp
        import numpy as np
        GROUP = 64
        MAX_REL = 32

        def _silu(x):
            return x * jax.nn.sigmoid(x)

        def _ln(x, w, b, eps=1e-05):
            m = x.mean(-1, keepdims=True)
            v = ((x - m) ** 2).mean(-1, keepdims=True)
            return (x - m) / jnp.sqrt(v + eps) * w + b

        def _rope(x):
            n, d = (x.shape[-2], x.shape[-1])
            half = d // 2
            pos = jnp.arange(n, dtype=x.dtype)
            inv_freq = 10000.0 ** (-jnp.arange(half, dtype=x.dtype) / half)
            sinusoid = pos[:, None] * inv_freq[None, :]
            sin, cos = (jnp.sin(sinusoid), jnp.cos(sinusoid))
            x1, x2 = (x[..., :half], x[..., half:])
            return jnp.concatenate([x1 * cos - x2 * sin, x2 * cos + x1 * sin], axis=-1)
        key = jax.random.key(seed)
        ks = jax.random.split(key, 8)
        B, N, D, QK, H = (4, 512, 128, 32, 256)
        s = 0.02
        return {'x': jax.random.normal(ks[0], (B, N, D), dtype=jnp.float32), 'ln1_w': jnp.ones((D,), jnp.float32), 'ln1_b': jnp.zeros((D,), jnp.float32), 'Wqk': jax.random.normal(ks[1], (QK, D), jnp.float32) * s, 'bqk': jnp.zeros((QK,), jnp.float32), 'Wv': jax.random.normal(ks[2], (H, D), jnp.float32) * s, 'bv': jnp.zeros((H,), jnp.float32), 'Wg': jax.random.normal(ks[3], (H, D), jnp.float32) * s, 'bg': jnp.zeros((H,), jnp.float32), 'Wo': jax.random.normal(ks[4], (D, H), jnp.float32) * s, 'bo': jnp.zeros((D,), jnp.float32), 'ln2_w': jnp.ones((D,), jnp.float32), 'ln2_b': jnp.zeros((D,), jnp.float32), 'gamma': jax.random.normal(ks[5], (4, QK), jnp.float32) * 0.02, 'beta': jnp.zeros((4, QK), jnp.float32), 'pos_emb': jax.random.normal(ks[6], (2 * MAX_REL + 1,), jnp.float32)}
    _L0_attn_in = _L0_attn_setup()

    def _L0_ffn_setup():
        import jax, jax.numpy as jnp
        import numpy as np
        DIM = 128

        def _reference_tuple_inner(x, W_r, W_k, W_v, mu_r, mu_k):
            B, T, C = x.shape
            x_prev = jnp.concatenate([jnp.zeros((B, 1, C), x.dtype), x[:, :-1, :]], axis=1)
            xr = mu_r * x + (1.0 - mu_r) * x_prev
            xk = mu_k * x + (1.0 - mu_k) * x_prev
            r = jax.nn.sigmoid(jnp.einsum('btc,dc->btd', xr, W_r))
            k = jnp.einsum('btc,dc->btd', xk, W_k)
            k_act = jnp.square(jax.nn.relu(k))
            out = r * jnp.einsum('btc,dc->btd', k_act, W_v)
            new_state = x[:, -1, :]
            return (out, new_state)
        key = jax.random.key(seed)
        ks = jax.random.split(key, 6)
        B, T, C = (8, 256, DIM)
        x = jax.random.normal(ks[0], (B, T, C), dtype=jnp.float32)
        s = 1.0 / np.sqrt(C)
        W_r = jax.random.uniform(ks[1], (C, C), jnp.float32, -s, s)
        W_k = jax.random.uniform(ks[2], (C, C), jnp.float32, -s, s)
        W_v = jax.random.uniform(ks[3], (C, C), jnp.float32, -s, s)
        mu_r = jax.random.uniform(ks[4], (C,), jnp.float32)
        mu_k = jax.random.uniform(ks[5], (C,), jnp.float32)
        return {'x': x, 'W_r': W_r, 'W_k': W_k, 'W_v': W_v, 'mu_r': mu_r, 'mu_k': mu_k}
    _L0_ffn_in = _L0_ffn_setup()
    _d = {'L0_attn_x': _L0_attn_in['x'], 'L0_attn_ln1_w': _L0_attn_in['ln1_w'], 'L0_attn_ln1_b': _L0_attn_in['ln1_b'], 'L0_attn_Wqk': _L0_attn_in['Wqk'], 'L0_attn_bqk': _L0_attn_in['bqk'], 'L0_attn_Wv': _L0_attn_in['Wv'], 'L0_attn_bv': _L0_attn_in['bv'], 'L0_attn_Wg': _L0_attn_in['Wg'], 'L0_attn_bg': _L0_attn_in['bg'], 'L0_attn_Wo': _L0_attn_in['Wo'], 'L0_attn_bo': _L0_attn_in['bo'], 'L0_attn_ln2_w': _L0_attn_in['ln2_w'], 'L0_attn_ln2_b': _L0_attn_in['ln2_b'], 'L0_attn_gamma': _L0_attn_in['gamma'], 'L0_attn_beta': _L0_attn_in['beta'], 'L0_attn_pos_emb': _L0_attn_in['pos_emb'], 'L0_ffn_W_r': _L0_ffn_in['W_r'], 'L0_ffn_W_k': _L0_ffn_in['W_k'], 'L0_ffn_W_v': _L0_ffn_in['W_v'], 'L0_ffn_mu_r': _L0_ffn_in['mu_r'], 'L0_ffn_mu_k': _L0_ffn_in['mu_k']}
    _x0 = _d['L0_attn_x']
    _d['L0_attn_x'] = jax.random.normal(jax.random.fold_in(jax.random.key(seed), 1), (16, 256, 128), dtype=_x0.dtype)
    del _x0
    return _d

def reference(L0_attn_x, L0_attn_ln1_w, L0_attn_ln1_b, L0_attn_Wqk, L0_attn_bqk, L0_attn_Wv, L0_attn_bv, L0_attn_Wg, L0_attn_bg, L0_attn_Wo, L0_attn_bo, L0_attn_ln2_w, L0_attn_ln2_b, L0_attn_gamma, L0_attn_beta, L0_attn_pos_emb, L0_ffn_W_r, L0_ffn_W_k, L0_ffn_W_v, L0_ffn_mu_r, L0_ffn_mu_k):

    def _L0_attn_ref(x, ln1_w, ln1_b, Wqk, bqk, Wv, bv, Wg, bg, Wo, bo, ln2_w, ln2_b, gamma, beta, pos_emb):
        import jax, jax.numpy as jnp
        import numpy as np
        GROUP = 64
        MAX_REL = 32

        def _silu(x):
            return x * jax.nn.sigmoid(x)

        def _ln(x, w, b, eps=1e-05):
            m = x.mean(-1, keepdims=True)
            v = ((x - m) ** 2).mean(-1, keepdims=True)
            return (x - m) / jnp.sqrt(v + eps) * w + b

        def _rope(x):
            n, d = (x.shape[-2], x.shape[-1])
            half = d // 2
            pos = jnp.arange(n, dtype=x.dtype)
            inv_freq = 10000.0 ** (-jnp.arange(half, dtype=x.dtype) / half)
            sinusoid = pos[:, None] * inv_freq[None, :]
            sin, cos = (jnp.sin(sinusoid), jnp.cos(sinusoid))
            x1, x2 = (x[..., :half], x[..., half:])
            return jnp.concatenate([x1 * cos - x2 * sin, x2 * cos + x1 * sin], axis=-1)
        b, n, d = x.shape
        G = GROUP
        x = _ln(x, ln1_w, ln1_b)
        qk = _silu(x @ Wqk.T + bqk)
        v = _silu(x @ Wv.T + bv)
        heads = qk[..., None, :] * gamma + beta
        quad_q, lin_q, quad_k, lin_k = (heads[..., i, :] for i in range(4))
        quad_q, lin_q, quad_k, lin_k = map(_rope, (quad_q, lin_q, quad_k, lin_k))
        g = n // G
        rs = lambda t: t.reshape(b, g, G, t.shape[-1])
        qq, lq, qkk, lk, vg = map(rs, (quad_q, lin_q, quad_k, lin_k, v))
        idx = jnp.arange(G)
        dist = jnp.clip(jnp.abs(idx[:, None] - idx[None, :]), 0, MAX_REL)
        bias = pos_emb[dist]
        quad_att = jnp.einsum('bgid,bgjd->bgij', qq, qkk) / G + bias
        attn = jax.nn.relu(quad_att) ** 2
        quad_out = jnp.einsum('bgij,bgje->bgie', attn, vg)
        lin_kv = jnp.einsum('bgnd,bgne->bde', lk, vg) / n
        lin_out = jnp.einsum('bgnd,bde->bgne', lq, lin_kv)
        qo = quad_out.reshape(b, n, -1)
        lo = lin_out.reshape(b, n, -1)
        gate = _silu(x @ Wg.T + bg)
        out = gate * (qo + lo)
        out = out @ Wo.T + bo
        return _ln(out, ln2_w, ln2_b)

    def _L0_ffn_ref(x, W_r, W_k, W_v, mu_r, mu_k):
        import jax, jax.numpy as jnp
        import numpy as np
        DIM = 128

        def _reference_tuple_inner(x, W_r, W_k, W_v, mu_r, mu_k):
            B, T, C = x.shape
            x_prev = jnp.concatenate([jnp.zeros((B, 1, C), x.dtype), x[:, :-1, :]], axis=1)
            xr = mu_r * x + (1.0 - mu_r) * x_prev
            xk = mu_k * x + (1.0 - mu_k) * x_prev
            r = jax.nn.sigmoid(jnp.einsum('btc,dc->btd', xr, W_r))
            k = jnp.einsum('btc,dc->btd', xk, W_k)
            k_act = jnp.square(jax.nn.relu(k))
            out = r * jnp.einsum('btc,dc->btd', k_act, W_v)
            new_state = x[:, -1, :]
            return (out, new_state)
        return _reference_tuple_inner(x, W_r, W_k, W_v, mu_r, mu_k)[0]
    x = L0_attn_x
    xn = _layernorm(x, axis=-1)
    x = x + _L0_attn_ref(xn, L0_attn_ln1_w, L0_attn_ln1_b, L0_attn_Wqk, L0_attn_bqk, L0_attn_Wv, L0_attn_bv, L0_attn_Wg, L0_attn_bg, L0_attn_Wo, L0_attn_bo, L0_attn_ln2_w, L0_attn_ln2_b, L0_attn_gamma, L0_attn_beta, L0_attn_pos_emb) + _L0_ffn_ref(xn, L0_ffn_W_r, L0_ffn_W_k, L0_ffn_W_v, L0_ffn_mu_r, L0_ffn_mu_k)
    return x

_drawn_inputs = setup_inputs


def setup_inputs(seed=0):
    import zlib

    import numpy as np

    out = dict(_drawn_inputs(seed))
    spreads = {'L0_attn_ln1_w': (1.0, 0.2),
     'L0_attn_ln1_b': (0.0, 0.1),
     'L0_attn_bqk': (0.0, 2.0),
     'L0_attn_bv': (0.0, 0.1),
     'L0_attn_bg': (0.0, 0.1),
     'L0_attn_bo': (0.0, 0.1),
     'L0_attn_ln2_w': (1.0, 0.2),
     'L0_attn_ln2_b': (0.0, 0.1),
     'L0_attn_beta': (0.0, 2.0)}
    factors = {'L0_attn_Wqk': 46.941, 'L0_attn_gamma': 28.027, 'L0_ffn_W_r': 4.546, 'L0_ffn_mu_r': 8.0}
    for name, (base, spread) in spreads.items():
        noise = np.random.default_rng([zlib.crc32(name.encode()), seed]).standard_normal(out[name].shape)
        drawn = base * np.exp(spread * noise) if base else spread * noise
        out[name] = jnp.asarray(drawn.astype(out[name].dtype))
    for name, factor in factors.items():
        out[name] = (out[name] * factor).astype(out[name].dtype)
    return out
```

```python
from contextlib import ExitStack

import concourse.bass as bass
from concourse import mybir

ALU = mybir.AluOpType
ACT = mybir.ActivationFunctionType
F32 = mybir.dt.float32
BF16 = mybir.dt.bfloat16

P = 128
SEQ = 256
D = 128
QK = 32
E = 256
EC = E // P
GROUP = 64
UNIT = 512
NB = UNIT // SEQ
NT = UNIT // P
MAX_REL = 32
EPS = 1e-5

W_QK, W_V, W_G, W_O, W_R, W_K, W_F = 0, 64, 320, 576, 832, 960, 1088
W_ALL = 1216
V_LN1W, V_LN1B, V_MUR, V_MUK, V_BG, V_BQK, V_HEADS = 0, 1, 2, 3, 4, 6, 7
V_ALL = 11
C_ID, C_ROPE, C_HEADEYE, C_MASK, C_SEL, C_SPLIT = 0, 128, 384, 416, 544, 672
C_ALL = 675


def block_kernel(nc, x, weights, vectors, bv, bo, ln2_w, ln2_b, pos_emb, consts, out):
    tokens = x.shape[0] * x.shape[1]
    units = tokens // UNIT
    assert x.shape[1] == SEQ and tokens % UNIT == 0 and units % 2 == 0 and units >= 4
    x_units = x.rearrange("(u b) (t p) d -> u p (b t) d", b=NB, p=P)
    out_units = out.rearrange("(u b) (t p) d -> u p (b t) d", b=NB, p=P)
    scratch = nc.dram_tensor("bias_rows", (GROUP, P), F32, kind="Internal").ap()

    with ExitStack() as ctx:
        def sb(name, shape, dt=F32):
            return ctx.enter_context(nc.sbuf_tensor(name, shape, dt))

        def sem(name):
            return ctx.enter_context(nc.semaphore(name))

        w = sb("w", [P, W_ALL])
        vec = sb("vec", [P, V_ALL])
        cst = sb("cst", [P, C_ALL])
        brow = sb("brow", [P, E + D])
        bhi = sb("bhi", [P, E + D], BF16)
        bmid = sb("bmid", [P, E + D], BF16)
        brest = sb("brest", [P, E + D])
        brest2 = sb("brest2", [P, E + D])
        bsum = sb("bsum", [P, E + D])
        bsum2 = sb("bsum2", [P, E + D])
        bv3 = sb("bv3", [P, 2, E], BF16)
        bo3 = sb("bo3", [P, NT, D], BF16)
        ones = sb("ones", [P, P], BF16)
        ln2w = sb("ln2w", [P, D])
        ln2b = sb("ln2b", [P, D])
        pos = sb("pos", [2 * MAX_REL + 1, 1])
        posb = sb("posb", [2 * MAX_REL + 1, GROUP])
        biasrow = sb("biasrow", [GROUP, P])
        bias = sb("bias", [P, P])
        heads = sb("heads", [P, 4 * QK])
        mhalf = sb("mhalf", [P, NT])
        eps = sb("eps", [P, NT])
        wf = sb("wf", [P, D])

        X = [sb(f"X{p}", [P, NT, D]) for p in range(2)]
        st = sb("st", [P, NT, 6])
        mv = sb("mv", [P, NT, 2])
        var1 = sb("var1", [P, NT])
        rstd1 = sb("rstd1", [P, NT])
        var2a = sb("var2a", [P, NT])
        var2b = sb("var2b", [P, NT])
        var2 = sb("var2", [P, NT])
        rstd12a = sb("rstd12a", [P, NT])
        rstd12 = sb("rstd12", [P, NT])
        xn = sb("xn", [P, NT, D])
        xa = sb("xa", [P, NT, D])
        xnT = sb("xnT", [P, NB, SEQ + 1])
        xaT = sb("xaT", [P, UNIT])
        step = sb("step", [P, NB, SEQ])
        xr = sb("xr", [P, NB, SEQ])
        xk = sb("xk", [P, NB, SEQ])
        kr = sb("kr", [P, UNIT])
        kact = sb("kact", [P, UNIT])
        rt = sb("rt", [P, UNIT])
        ffn = sb("ffn", [P, UNIT])
        xb = sb("xb", [P, NT, D])
        rest = sb("rest", [P, UNIT])
        s = sb("s", [2 * QK, UNIT])
        Z = sb("Z", [P, NB, SEQ])
        q = sb("q", [2 * QK, UNIT])
        k = sb("k", [QK, UNIT])
        lk = sb("lk", [P, NT, QK])
        v = sb("v", [P, NT, E])
        g = [sb(f"g{p}", [P, EC, UNIT]) for p in range(2)]
        a1 = sb("a1", [P, NT, P])
        a2 = sb("a2", [P, NT, P])
        kvT = sb("kvT", [P, NB * EC, QK])
        kv = sb("kv", [2 * QK, NB, E])
        gated = sb("gated", [P, EC, UNIT])
        st2 = sb("st2", [P, NT, 6])
        mv2 = sb("mv2", [P, NT, 2])
        var3 = sb("var3", [P, NT])
        rstd3 = sb("rstd3", [P, NT])
        o1 = sb("o1", [P, NT, D])
        Y = sb("Y", [P, NT, D])

        ps = ctx.enter_context(nc.psum_tensor("ps", [P, 8, 512], F32))
        ident = cst[:, C_ID:C_ID + P]
        rope = cst[:, C_ROPE:C_ROPE + SEQ]
        p_lk = p_kvT = p_qk = ps[:, 0, :]
        p_heads = p_k = p_kv = ps[:, 1, :]
        p_r = p_o = ps[:, 2, :]
        p_att = p_v = ps[:, 3:5, :]
        p_scores = p_ffn = ps[:, 5, :]
        p_xn, p_xa = ps[:, 6, :], ps[:, 7, :]
        p_g = ps[:, 6:8, :]

        w_loaded, vec_loaded, cst_loaded = sem("w_loaded"), sem("vec_loaded"), sem("cst_loaded")
        brow_loaded, ln2_loaded, pos_loaded = sem("brow_loaded"), sem("ln2_loaded"), sem("pos_loaded")
        biasrow_stored, bias_loaded = sem("biasrow_stored"), sem("bias_loaded")
        x_loaded = [sem(f"x_loaded{p}") for p in range(2)]
        y_stored = sem("y_stored")
        setup_dve, setup_pe, setup_pool = sem("setup_dve"), sem("setup_pe"), sem("setup_pool")
        split_step = sem("split_step")
        stats_ready, aggr_ready = sem("stats_ready"), sem("aggr_ready")
        pool_small = sem("pool_small")
        rstd1_ready, rstd3_ready = sem("rstd1_ready"), sem("rstd3_ready")
        xn_ready, xT_done = sem("xn_ready"), sem("xT_done")
        xaT_ready, xnT_ready = sem("xaT_ready"), sem("xnT_ready")
        step_ready, mix_ready = sem("step_ready"), sem("mix_ready")
        qk_done, s_ready, Z_ready = sem("qk_done"), sem("s_ready"), sem("Z_ready")
        heads_done, lk_done = sem("heads_done"), sem("lk_done")
        q_ready, lk_ready = sem("q_ready"), sem("lk_ready")
        g_done, g_ready, v_done, v_ready = sem("g_done"), sem("g_ready"), sem("v_done"), sem("v_ready")
        scores_done, a1_ready, a2_ready = sem("scores_done"), sem("a1_ready"), sem("a2_ready")
        k_done, kr_ready, kact_ready = sem("k_done"), sem("kr_ready"), sem("kact_ready")
        r_done, rt_ready = sem("r_done"), sem("rt_ready")
        ffnv_done, ffn_ready, xb_ready, rest_ready = (
            sem("ffnv_done"), sem("ffn_ready"), sem("xb_ready"), sem("rest_ready"))
        kvT_done, kvT_ready, kv_done, kv_ready = (
            sem("kvT_done"), sem("kvT_ready"), sem("kv_done"), sem("kv_ready"))
        att_done, gated_ready, o_done = sem("att_done"), sem("gated_ready"), sem("o_done")
        stats3_ready, aggr3_ready, o1_ready, y_ready = (
            sem("stats3_ready"), sem("aggr3_ready"), sem("o1_ready"), sem("y_ready"))

        block = ctx.enter_context(nc.Block())

        def later(u):
            return not isinstance(u, int) or u > 0

        def pipeline(eng, first, slot):
            first()
            slot(0, 0, True)
            with eng.Fori(0, units // 2 - 1) as j:
                slot(j, 1, True)
                slot(j + 1, 0, True)
            slot(units // 2 - 1, 1, False)

        def following(i, p):
            return (i, 1) if p == 0 else (i + 1, 0)

        @block.sync
        def _(sp):
            sp.dma_start(X[0][:], x_units[0]).then_inc(x_loaded[0], 16)
            sp.dma_start(w[:], weights).then_inc(w_loaded, 16)
            sp.dma_start(X[1][:], x_units[1]).then_inc(x_loaded[1], 16)
            sp.wait_ge(setup_dve, 2)
            sp.dma_start(scratch, biasrow[:]).then_inc(biasrow_stored, 16)
            sp.wait_ge(biasrow_stored, 16)
            skewed = bass.AP(scratch.tensor, GROUP - 1, [[P - 1, GROUP], [1, GROUP]])
            sp.wait_ge(setup_dve, 3)
            for h in range(P // GROUP):
                at = slice(h * GROUP, (h + 1) * GROUP)
                sp.dma_start(bias[at, at], skewed).then_inc(bias_loaded, 16)

            def slot(i, p, load):
                u = i * 2 + p
                if load:
                    sp.wait_ge(xb_ready, u + 1)
                    sp.dma_start(X[p][:], x_units[u + 2]).then_inc(x_loaded[p], 16)
                sp.wait_ge(y_ready, NT * (u + 1))
                sp.dma_start(out_units[u], Y[:]).then_inc(y_stored, 16)

            slot(0, 0, True)
            with sp.Fori(0, units // 2 - 2) as j:
                slot(j, 1, True)
                slot(j + 1, 0, True)
            slot(units // 2 - 2, 1, True)
            slot(units // 2 - 1, 0, False)
            slot(units // 2 - 1, 1, False)
            sp.wait_ge(y_stored, 16 * units)

        @block.gpsimd
        def _(pool):
            pool.memset(mhalf[:], -0.5).then_inc(setup_pool, 1)
            pool.memset(eps[:], EPS).then_inc(setup_pool, 1)
            pool.memset(ones[:], 1.0).then_inc(setup_pool, 1)
            for b in range(NB):
                pool.memset(xnT[:, b, 0:1], 0.0).then_inc(setup_pool, 1)
            pool.wait_ge(setup_pool, 3 + NB)
            pool.wait_ge(cst_loaded, 16)

            def rstds(i, p, n):
                base = n * 5
                pool.wait_ge(aggr_ready, NT * (n + 1))
                pool.tensor_tensor(var1[:], mv[:, :, 1], eps[:], ALU.add).then_inc(pool_small, 1)
                pool.wait_ge(pool_small, base + 1)
                if later(n):
                    pool.wait_ge(xn_ready, n)
                pool.tensor_tensor(rstd1[:], var1[:], mhalf[:], ALU.pow).then_inc(pool_small, 1)
                pool.wait_ge(pool_small, base + 2)
                pool.tensor_tensor(var2a[:], rstd1[:], rstd1[:], ALU.mult).then_inc(pool_small, 1)
                pool.wait_ge(pool_small, base + 3)
                pool.tensor_tensor(var2b[:], var2a[:], mv[:, :, 1], ALU.mult).then_inc(pool_small, 1)
                pool.wait_ge(pool_small, base + 4)
                pool.tensor_tensor(var2[:], var2b[:], eps[:], ALU.add).then_inc(pool_small, 1)
                pool.wait_ge(pool_small, base + 5)
                pool.tensor_tensor(rstd12a[:], var2[:], mhalf[:], ALU.pow).then_inc(rstd1_ready, 1)
                pool.wait_ge(rstd1_ready, 2 * n + 1)
                pool.tensor_tensor(rstd12[:], rstd12a[:], rstd1[:], ALU.mult).then_inc(rstd1_ready, 1)

            def rotate(n):
                pool.wait_ge(s_ready, n + 1)
                if later(n):
                    pool.wait_ge(lk_done, n)
                pool.tensor_tensor(Z[0:2 * QK, :, :], s[:].rearrange("p (b n) -> p b n", b=NB),
                                   rope[0:2 * QK, :].unsqueeze(1).to_broadcast([2 * QK, NB, SEQ]),
                                   ALU.mult).then_inc(Z_ready, 1)

            def shift(n):
                pool.wait_ge(xnT_ready, n + 1)
                if later(n):
                    pool.wait_ge(mix_ready, 2 * n)
                pool.tensor_tensor(step[:], xnT[:, :, 1:SEQ + 1], xnT[:, :, 0:SEQ],
                                   ALU.subtract).then_inc(step_ready, 1)

            def first():
                rstds(0, 0, 0)
                rotate(0)
                shift(0)

            def slot(i, p, more):
                u = i * 2 + p
                if more:
                    rstds(i, p, u + 1)
                pool.wait_ge(kr_ready, u + 1)
                if later(u):
                    pool.wait_ge(ffnv_done, u)
                pool.tensor_tensor(kact[:], kr[:], kr[:], ALU.mult).then_inc(kact_ready, 1)
                pool.wait_ge(ln2_loaded, 32)
                pool.wait_ge(x_loaded[p], 16 * (i + 1))
                if later(u):
                    pool.wait_ge(rest_ready, u)
                pool.tensor_tensor(xb[:], X[p][:], ln2b[:].unsqueeze(1).to_broadcast([P, NT, D]),
                                   ALU.add).then_inc(xb_ready, 1)
                pool.wait_ge(ffn_ready, u + 1)
                pool.wait_ge(xb_ready, u + 1)
                if later(u):
                    pool.wait_ge(y_ready, NT * u)
                pool.tensor_tensor(rest[:], ffn[:], xb[:].rearrange("p t d -> p (t d)"),
                                   ALU.add).then_inc(rest_ready, 1)
                if more:
                    rotate(u + 1)
                    shift(u + 1)
                pool.wait_ge(aggr3_ready, NT * (u + 1))
                pool.tensor_tensor(var3[:], mv2[:, :, 1], eps[:], ALU.add).then_inc(rstd3_ready, 1)
                pool.wait_ge(rstd3_ready, 2 * u + 1)
                if later(u):
                    pool.wait_ge(y_ready, NT * u)
                pool.tensor_tensor(rstd3[:], var3[:], mhalf[:], ALU.pow).then_inc(rstd3_ready, 1)

            pipeline(pool, first, slot)

        @block.vector
        def _(dve):
            def put(ins, n):
                ins.then_inc(split_step, 1)
                dve.wait_ge(split_step, n)

            def biases():
                dve.wait_ge(brow_loaded, 32)
                put(dve.tensor_copy(bhi[:], brow[:]), 1)
                put(dve.tensor_tensor(brest[:], brow[:], bhi[:], ALU.subtract), 2)
                put(dve.tensor_copy(bmid[:], brest[:]), 3)
                put(dve.tensor_tensor(brest2[:], brest[:], bmid[:], ALU.subtract), 4)
                split = cst[:, C_SPLIT:C_SPLIT + 3]
                put(dve.tensor_scalar(bsum[:], bhi[:], split[:, 0:1], None, ALU.mult), 5)
                put(dve.scalar_tensor_tensor(out=bsum2[:], in0=bmid[:], scalar=split[:, 1:2],
                                             in1=bsum[:], op0=ALU.mult, op1=ALU.add), 6)
                put(dve.scalar_tensor_tensor(out=bsum[:], in0=brest2[:], scalar=split[:, 2:3],
                                             in1=bsum2[:], op0=ALU.mult, op1=ALU.add), 7)
                dve.tensor_copy(bv3[:], bsum[:, 0:E].unsqueeze(1).to_broadcast([P, 2, E])
                                ).then_inc(setup_dve, 1)
                dve.wait_ge(w_loaded, 16)
                dve.tensor_scalar(wf[:], w[:, W_F:W_F + D], 0.5, None, ALU.mult).then_inc(setup_dve, 1)
                dve.tensor_copy(bo3[:], bsum[:, E:E + D].unsqueeze(1).to_broadcast([P, NT, D])
                                ).then_inc(setup_dve, 1)

            def head_matrix():
                dve.wait_ge(cst_loaded, 16)
                dve.wait_ge(vec_loaded, 16)
                for h in range(4):
                    dve.tensor_scalar(heads[:, h * QK:(h + 1) * QK], cst[:, C_HEADEYE:C_HEADEYE + QK],
                                      vec[:, V_HEADS + h:V_HEADS + h + 1], None, ALU.mult
                                      ).then_inc(setup_dve, 1)
                for b in range(NB):
                    dve.tensor_copy(Z[2 * QK:P, b, :], rope[2 * QK:P, :]).then_inc(setup_dve, 1)

            def position_bias():
                dve.wait_ge(pos_loaded, 16)
                dve.tensor_scalar(posb[:], cst[0:2 * MAX_REL + 1, C_ID:C_ID + GROUP], 0.0,
                                  pos[:, 0:1], ALU.mult, ALU.add).then_inc(setup_dve, 1)
                dve.wait_ge(setup_pe, 1)
                dve.tensor_copy(biasrow[:], p_scores[0:GROUP, 0:P]).then_inc(setup_dve, 1)
                dve.tensor_copy(bias[:], cst[:, C_MASK:C_MASK + P]).then_inc(setup_dve, 1)

            def stats(i, p, n):
                dve.wait_ge(x_loaded[p], 16 * (i + 1))
                for t in range(NT):
                    dve.bn_stats(st[:, t, :], X[p][:, t, :]).then_inc(stats_ready, 1)

            def aggregate():
                for t in range(NT):
                    dve.bn_aggr(mv[:, t, :], st[:, t, :]).then_inc(aggr_ready, 1)

            def norm(p, n):
                dve.wait_ge(rstd1_ready, 2 * (n + 1))
                if later(n):
                    dve.wait_ge(xT_done, n)
                for t in range(NT):
                    dve.tensor_scalar(xa[:, t, :], X[p][:, t, :], mv[:, t, 0:1], rstd12[:, t:t + 1],
                                      ALU.subtract, ALU.mult)
                for t in range(NT):
                    last = dve.tensor_scalar(xn[:, t, :], X[p][:, t, :], mv[:, t, 0:1],
                                             rstd1[:, t:t + 1], ALU.subtract, ALU.mult)
                last.then_inc(xn_ready, 1)

            def mix(n):
                dve.wait_ge(step_ready, n + 1)
                if later(n):
                    dve.wait_ge(r_done, n)
                for dst, mu in ((xk, V_MUK), (xr, V_MUR)):
                    dve.scalar_tensor_tensor(out=dst[:], in0=step[:], scalar=vec[:, mu:mu + 1],
                                             in1=xnT[:, :, 0:SEQ], op0=ALU.mult, op1=ALU.add
                                             ).then_inc(mix_ready, 1)

            def linear_keys(n):
                dve.wait_ge(lk_done, n + 1)
                if later(n):
                    dve.wait_ge(kvT_done, n)
                dve.tensor_copy(lk[:].rearrange("p t d -> p (t d)"), p_lk[:, 0:NT * QK]
                                ).then_inc(lk_ready, 1)

            def first():
                stats(0, 0, 0)
                dve.wait_ge(stats_ready, NT)
                aggregate()
                position_bias()
                head_matrix()
                biases()
                norm(0, 0)
                mix(0)
                linear_keys(0)

            def slot(i, p, more):
                u = i * 2 + p
                if more:
                    ni, np_ = following(i, p)
                    stats(ni, np_, u + 1)
                if more:
                    dve.wait_ge(stats_ready, NT * (u + 2))
                dve.wait_ge(bias_loaded, 32)
                dve.wait_ge(scores_done, u + 1)
                dve.scalar_tensor_tensor(out=a1[:], in0=p_scores.rearrange("p (t j) -> p t j", t=NT),
                                         scalar=1.0 / GROUP,
                                         in1=bias[:].unsqueeze(1).to_broadcast([P, NT, P]),
                                         op0=ALU.mult, op1=ALU.add).then_inc(a1_ready, 1)
                if more:
                    aggregate()
                dve.wait_ge(a1_ready, u + 1)
                if later(u):
                    dve.wait_ge(att_done, 2 * u)
                dve.scalar_tensor_tensor(out=a2[:], in0=a1[:], scalar=0.0, in1=a1[:],
                                         op0=ALU.max, op1=ALU.mult).then_inc(a2_ready, 1)
                if more:
                    norm(np_, u + 1)
                dve.wait_ge(kvT_done, u + 1)
                if later(u):
                    dve.wait_ge(kv_done, u)
                dve.tensor_copy(kvT[:].rearrange("p c d -> p (c d)"), p_kvT[:, 0:NB * EC * QK]
                                ).then_inc(kvT_ready, 1)
                dve.wait_ge(ffnv_done, u + 1)
                dve.wait_ge(rt_ready, u + 1)
                if later(u):
                    dve.wait_ge(rest_ready, u)
                dve.scalar_tensor_tensor(out=ffn[:], in0=rt[:], scalar=1.0, in1=p_ffn,
                                         op0=ALU.add, op1=ALU.mult).then_inc(ffn_ready, 1)
                for c in range(EC):
                    dve.wait_ge(att_done, 2 * u + c + 1)
                    dve.wait_ge(g_ready, EC * u + c + 1)
                    if later(u):
                        dve.wait_ge(o_done, u)
                    dve.tensor_tensor(gated[:, c, :], p_att[:, c, :], g[p][:, c, :], ALU.mult
                                      ).then_inc(gated_ready, 1)
                if more:
                    mix(u + 1)
                dve.wait_ge(o_done, u + 1)
                for t in range(NT):
                    dve.bn_stats(st2[:, t, :], p_o[:, t * D:(t + 1) * D]).then_inc(stats3_ready, 1)
                dve.wait_ge(stats3_ready, NT * (u + 1))
                if more:
                    linear_keys(u + 1)
                for t in range(NT):
                    dve.bn_aggr(mv2[:, t, :], st2[:, t, :]).then_inc(aggr3_ready, 1)
                dve.wait_ge(ln2_loaded, 32)
                dve.wait_ge(aggr3_ready, NT * (u + 1))
                for t in range(NT):
                    dve.scalar_tensor_tensor(out=o1[:, t, :], in0=p_o[:, t * D:(t + 1) * D],
                                             scalar=mv2[:, t, 0:1], in1=ln2w[:],
                                             op0=ALU.subtract, op1=ALU.mult).then_inc(o1_ready, 1)
                dve.wait_ge(rstd3_ready, 2 * (u + 1))
                dve.wait_ge(rest_ready, u + 1)
                if later(u):
                    dve.wait_ge(y_stored, 16 * u)
                for t in range(NT):
                    dve.wait_ge(o1_ready, NT * u + t + 1)
                    dve.scalar_tensor_tensor(out=Y[:, t, :], in0=o1[:, t, :],
                                             scalar=rstd3[:, t:t + 1], in1=rest[:, t * D:(t + 1) * D],
                                             op0=ALU.mult, op1=ALU.add).then_inc(y_ready, 1)

            pipeline(dve, first, slot)

        @block.scalar
        def _(act):
            act.dma_start(cst[:], consts).then_inc(cst_loaded, 16)
            act.dma_start(vec[:], vectors).then_inc(vec_loaded, 16)
            act.dma_start(pos[:], pos_emb.unsqueeze(1)).then_inc(pos_loaded, 16)
            act.dma_start(brow[:, 0:E], bv.unsqueeze(0).to_broadcast([P, E])).then_inc(brow_loaded, 16)
            act.dma_start(brow[:, E:E + D], bo.unsqueeze(0).to_broadcast([P, D])).then_inc(brow_loaded, 16)
            act.dma_start(ln2w[:], ln2_w.unsqueeze(0).to_broadcast([P, D])).then_inc(ln2_loaded, 16)
            act.dma_start(ln2b[:], ln2_b.unsqueeze(0).to_broadcast([P, D])).then_inc(ln2_loaded, 16)

            def column(c, rows=P):
                return vec[0:rows, c:c + 1]

            def transposed(n):
                act.wait_ge(xT_done, n + 1)
                if later(n):
                    act.wait_ge(v_done, n)
                act.activation(xaT[:], p_xa, ACT.Identity, bias=column(V_LN1B), scale=column(V_LN1W)
                               ).then_inc(xaT_ready, 1)
                if later(n):
                    act.wait_ge(mix_ready, 2 * n)
                act.activation(xnT[:, :, 1:SEQ + 1], p_xn.rearrange("p (b n) -> p b n", b=NB),
                               ACT.Identity).then_inc(xnT_ready, 1)

            def silu_qk(n):
                act.wait_ge(qk_done, n + 1)
                if later(n):
                    act.wait_ge(Z_ready, n)
                act.activation(s[:], p_qk[0:2 * QK, :], ACT.Silu, bias=column(V_BQK, 2 * QK)
                               ).then_inc(s_ready, 1)

            def silu_gate(p, n):
                for c in range(EC):
                    act.wait_ge(g_done, EC * n + c + 1)
                    if c == 0 and later(n) and later(n - 1):
                        act.wait_ge(gated_ready, EC * (n - 1))
                    act.activation(g[p][:, c, :], p_g[:, c, :], ACT.Silu, bias=column(V_BG + c)
                                   ).then_inc(g_ready, 1)

            def queries_keys(n):
                act.wait_ge(heads_done, n + 1)
                if later(n):
                    act.wait_ge(att_done, 2 * n)
                act.activation(k[:], p_heads[2 * QK:3 * QK, :], ACT.Identity).then_inc(q_ready, 1)
                act.activation(q[:], p_heads[0:2 * QK, :], ACT.Identity).then_inc(q_ready, 1)

            def silu_values(n):
                for h in range(2):
                    act.wait_ge(v_done, n + 1)
                    if later(n):
                        act.wait_ge(att_done, 2 * n)
                    act.activation(v[:, 2 * h:2 * h + 2, :].rearrange("p t e -> p (t e)"),
                                   p_v[:, h, :], ACT.Silu).then_inc(v_ready, 1)

            def first():
                act.wait_ge(vec_loaded, 16)
                transposed(0)
                silu_qk(0)
                silu_gate(0, 0)
                queries_keys(0)
                silu_values(0)

            def slot(i, p, more):
                u = i * 2 + p
                act.wait_ge(k_done, u + 1)
                if later(u):
                    act.wait_ge(kact_ready, u)
                act.activation(kr[:], p_k, ACT.Relu).then_inc(kr_ready, 1)
                act.wait_ge(r_done, u + 1)
                if later(u):
                    act.wait_ge(ffn_ready, u)
                act.activation(rt[:], p_r, ACT.Tanh, scale=0.5).then_inc(rt_ready, 1)
                if more:
                    transposed(u + 1)
                act.wait_ge(kv_done, u + 1)
                if later(u):
                    act.wait_ge(att_done, 2 * u)
                act.activation(kv[QK:2 * QK, :, :].rearrange("p b e -> p (b e)"), p_kv[0:QK, :],
                               ACT.Identity, scale=1.0 / SEQ).then_inc(kv_ready, 1)
                if more:
                    silu_qk(u + 1)
                    silu_gate(1 - p, u + 1)
                    queries_keys(u + 1)
                    silu_values(u + 1)

            pipeline(act, first, slot)

        @block.tensor
        def _(pe):
            pe.wait_ge(cst_loaded, 16)
            pe.wait_ge(setup_dve, 1)
            pe.matmul(p_scores[0:GROUP, 0:P], posb[:], cst[0:2 * MAX_REL + 1, C_SEL:C_SEL + P],
                      start=True, stop=True).then_inc(setup_pe, 1)

            def tile(t):
                return slice(t * P, (t + 1) * P)

            def transposes(n):
                pe.wait_ge(xn_ready, n + 1)
                if later(n):
                    pe.wait_ge(g_ready, EC * n)
                for t in range(NT):
                    pe.transpose(p_xa[:, tile(t)], xa[:, t, :], ident)
                for t in range(NT):
                    last = pe.transpose(p_xn[:, tile(t)], xn[:, t, :], ident)
                last.then_inc(xT_done, 1)

            def project_qk(n):
                pe.wait_ge(xaT_ready, n + 1)
                if later(n):
                    pe.wait_ge(kvT_ready, n)
                pe.matmul(p_qk[0:2 * QK, :], w[:, W_QK:W_QK + 2 * QK], xaT[:], start=True, stop=True
                          ).then_inc(qk_done, 1)

            def project_gate(n):
                pe.wait_ge(xnT_ready, n + 1)
                for c in range(EC):
                    pe.matmul(p_g[:, c, :], w[:, W_G + c * P:W_G + (c + 1) * P], xaT[:],
                              start=True, stop=True).then_inc(g_done, 1)

            def rotary_heads(n):
                pe.wait_ge(Z_ready, n + 1)
                z = Z[:].rearrange("p b n -> p (b n)")
                if later(n):
                    pe.wait_ge(kv_ready, n)
                pe.matmul(p_heads, heads[:], z, start=True, stop=True).then_inc(heads_done, 1)
                for t in range(NT):
                    last = pe.matmul(p_lk[:, t * QK:(t + 1) * QK], z[:, tile(t)],
                                     heads[:, 3 * QK:4 * QK], start=True, stop=True)
                last.then_inc(lk_done, 1)

            def project_values(n):
                if later(n):
                    pe.wait_ge(gated_ready, EC * n)
                for h in range(2):
                    pe.matmul(p_v[:, h, :], ones[:], bv3[:].rearrange("p a e -> p (a e)"),
                              start=True, stop=False, skip_group_check=True)
                    for t in range(2):
                        last = pe.matmul(p_v[:, h, t * E:(t + 1) * E], xaT[:, tile(2 * h + t)],
                                         w[:, W_V:W_V + E], start=False, stop=True,
                                         skip_group_check=True)
                last.then_inc(v_done, 1)

            def first():
                transposes(0)
                pe.wait_ge(w_loaded, 16)
                project_qk(0)
                project_gate(0)
                pe.wait_ge(setup_dve, 10 + NB)
                pe.wait_ge(setup_pool, 3 + NB)
                rotary_heads(0)
                project_values(0)

            def slot(i, p, more):
                u = i * 2 + p
                pe.wait_ge(q_ready, 2 * (u + 1))
                if later(u):
                    pe.wait_ge(ffn_ready, u)
                for t in range(NT):
                    last = pe.matmul(p_scores[:, tile(t)], k[0:QK, tile(t)], q[0:QK, tile(t)],
                                     start=True, stop=True)
                last.then_inc(scores_done, 1)
                pe.wait_ge(mix_ready, 2 * (u + 1))
                pe.matmul(p_k, w[:, W_K:W_K + D], xk[:].rearrange("p b n -> p (b n)"),
                          start=True, stop=True).then_inc(k_done, 1)
                if later(u):
                    pe.wait_ge(o1_ready, NT * u)
                for t in range(NT):
                    last = pe.matmul(p_r[:, tile(t)], xr[:].rearrange("p b n -> p (b n)")[:, tile(t)],
                                     w[:, W_R:W_R + D], start=True, stop=True)
                last.then_inc(r_done, 1)
                pe.wait_ge(v_ready, 2 * (u + 1))
                pe.wait_ge(lk_ready, u + 1)
                for b in range(NB):
                    for c in range(EC):
                        at = (b * EC + c) * QK
                        for t in range(2):
                            last = pe.matmul(p_kvT[:, at:at + QK], v[:, 2 * b + t, c * P:(c + 1) * P],
                                             lk[:, 2 * b + t, :], start=(t == 0), stop=(t == 1))
                last.then_inc(kvT_done, 1)
                pe.wait_ge(a2_ready, u + 1)
                for c in range(EC):
                    for t in range(NT):
                        pe.matmul(p_att[:, c, tile(t)], v[:, t, c * P:(c + 1) * P], a2[:, t, :],
                                  start=(t == 0), stop=False, skip_group_check=True)
                pe.wait_ge(kact_ready, u + 1)
                for t in range(NT):
                    last = pe.matmul(p_ffn[:, tile(t)], kact[:, tile(t)], wf[:],
                                     start=True, stop=True)
                last.then_inc(ffnv_done, 1)
                if more:
                    transposes(u + 1)
                pe.wait_ge(kvT_ready, u + 1)
                pe.wait_ge(kr_ready, u + 1)
                for b in range(NB):
                    for c in range(EC):
                        last = pe.transpose(p_kv[0:QK, b * E + c * P:b * E + (c + 1) * P],
                                            kvT[:, b * EC + c, :], ident)
                last.then_inc(kv_done, 1)
                if more:
                    project_qk(u + 1)
                pe.wait_ge(kv_ready, u + 1)
                for c in range(EC):
                    for b in range(NB):
                        last = pe.matmul(p_att[:, c, b * SEQ:(b + 1) * SEQ],
                                         kv[QK:2 * QK, b, c * P:(c + 1) * P],
                                         q[QK:2 * QK, b * SEQ:(b + 1) * SEQ],
                                         start=False, stop=True, skip_group_check=True)
                    last.then_inc(att_done, 1)
                if more:
                    project_gate(u + 1)
                pe.wait_ge(rt_ready, u + 1)
                pe.matmul(p_o, ones[:], bo3[:].rearrange("p t d -> p (t d)"),
                          start=True, stop=False, skip_group_check=True)
                pe.wait_ge(gated_ready, EC * (u + 1))
                for t in range(NT):
                    for c in range(EC):
                        last = pe.matmul(p_o[:, tile(t)], gated[:, c, tile(t)],
                                         w[:, W_O + c * D:W_O + (c + 1) * D], start=False,
                                         stop=(c == EC - 1), skip_group_check=True)
                last.then_inc(o_done, 1)
                if more:
                    rotary_heads(u + 1)
                    project_values(u + 1)

            pipeline(pe, first, slot)


def constants():
    import numpy as np
    half = QK // 2
    c = np.zeros((P, C_ALL), np.float32)
    c[:, C_ID:C_ID + P] = np.eye(P)
    inv = np.float32(10000.0) ** (-np.arange(half, dtype=np.float32) / np.float32(half))
    angle = np.arange(SEQ, dtype=np.float32)[None, :] * inv.astype(np.float32)[:, None]
    cos, sin = np.cos(angle.astype(np.float64)), np.sin(angle.astype(np.float64))
    table = np.concatenate([cos, cos, -sin, sin])
    c[:, C_ROPE:C_ROPE + SEQ] = np.concatenate([table, table])
    c[:, C_HEADEYE:C_HEADEYE + QK] = np.tile(np.eye(QK), (4, 1))
    block = np.arange(P) // GROUP
    c[:, C_MASK:C_MASK + P] = np.where(block[:, None] == block[None, :], 0.0, -3e38)
    away = np.minimum(np.abs(np.arange(P) - (GROUP - 1)), MAX_REL)
    c[:, C_SEL:C_SEL + P] = np.arange(P)[:, None] == away[None, :]
    c[0:3, C_SPLIT:C_SPLIT + 3] = np.eye(3)
    return c


def kernel(L0_attn_x, L0_attn_ln1_w, L0_attn_ln1_b, L0_attn_Wqk, L0_attn_bqk, L0_attn_Wv, L0_attn_bv,
           L0_attn_Wg, L0_attn_bg, L0_attn_Wo, L0_attn_bo, L0_attn_ln2_w, L0_attn_ln2_b, L0_attn_gamma,
           L0_attn_beta, L0_attn_pos_emb, L0_ffn_W_r, L0_ffn_W_k, L0_ffn_W_v, L0_ffn_mu_r, L0_ffn_mu_k):
    import numpy as np
    import concourse.bacc as bacc
    from concourse.bass_utils import run_bass_kernel_spmd

    x = np.ascontiguousarray(L0_attn_x)
    half = QK // 2
    swap = np.r_[half:QK, 0:half]
    wo = np.asarray(L0_attn_Wo).T
    weights = np.concatenate(
        [L0_attn_Wqk.T, np.asarray(L0_attn_Wqk)[swap].T, L0_attn_Wv.T, L0_attn_Wg.T, wo[:P], wo[P:],
         L0_ffn_W_r.T, L0_ffn_W_k.T, L0_ffn_W_v.T], axis=1)
    vectors = np.zeros((P, V_ALL), np.float32)
    vectors[:, V_LN1W] = L0_attn_ln1_w
    vectors[:, V_LN1B] = L0_attn_ln1_b
    vectors[:, V_MUR] = L0_ffn_mu_r
    vectors[:, V_MUK] = L0_ffn_mu_k
    vectors[:, V_BG:V_BG + EC] = np.asarray(L0_attn_bg).reshape(EC, P).T
    bqk, gamma, beta = np.asarray(L0_attn_bqk), np.asarray(L0_attn_gamma), np.asarray(L0_attn_beta)
    vectors[0:2 * QK, V_BQK] = np.concatenate([bqk, bqk[swap]])
    vectors[:, V_HEADS:V_HEADS + 4] = np.concatenate([gamma.T, gamma.T[swap], beta.T, beta.T[swap]])

    ins = {
        "x": x, "weights": np.ascontiguousarray(weights), "vectors": vectors,
        "bv": np.ascontiguousarray(L0_attn_bv), "bo": np.ascontiguousarray(L0_attn_bo),
        "ln2_w": np.ascontiguousarray(L0_attn_ln2_w), "ln2_b": np.ascontiguousarray(L0_attn_ln2_b),
        "pos_emb": np.ascontiguousarray(L0_attn_pos_emb), "consts": constants(),
    }
    nc = bacc.Bacc("TRN2", target_bir_lowering=False, num_devices=1)
    args = {name: nc.dram_tensor(f"in_{name}", a.shape, mybir.dt.from_np(a.dtype),
                                 kind="ExternalInput").ap() for name, a in ins.items()}
    out = nc.dram_tensor("out_y", x.shape, F32, kind="ExternalOutput").ap()
    block_kernel(nc, out=out, **args)
    r = run_bass_kernel_spmd(nc, [{f"in_{name}": a for name, a in ins.items()}], core_ids=[0])
    return r.results[0]["out_y"]
```

```python
from contextlib import ExitStack

import concourse.bass as bass
from concourse import mybir

ALU = mybir.AluOpType
ACT = mybir.ActivationFunctionType
F32 = mybir.dt.float32
F32R = mybir.dt.float32r
BF16 = mybir.dt.bfloat16

P = 128
SEQ = 256
D = 128
QK = 32
E = 256
EC = E // P
GROUP = 64
HG = P // GROUP
UNIT = 512
NB = UNIT // SEQ
NT = UNIT // P
MAX_REL = 32
EPS = 1e-5

W_QK, W_V, W_G, W_O, W_R, W_K, W_F = 0, 64, 320, 576, 832, 960, 1088
W_ALL = 1216
V_LN1W, V_LN1B, V_MUR, V_MUK, V_BG, V_BQK, V_HEADS = 0, 1, 2, 3, 4, 6, 7
V_ALL = 11
C_ID, C_ROPE, C_HEADEYE, C_SEL, C_SPLIT = 0, 128, 384, 416, 544
C_ALL = 547


def block_kernel(nc, x, weights, vectors, bv, bo, ln2_w, ln2_b, pos_emb, consts, out):
    tokens = x.shape[0] * x.shape[1]
    units = tokens // UNIT
    assert x.shape[1] == SEQ and tokens % UNIT == 0 and units % 2 == 0 and units >= 4
    x_units = x.rearrange("(u b) (t p) d -> u p (b t) d", b=NB, p=P)
    out_units = out.rearrange("(u b) (t p) d -> u p (b t) d", b=NB, p=P)
    scratch = nc.dram_tensor("bias_rows", (GROUP, P), F32, kind="Internal").ap()

    with ExitStack() as ctx:
        def sb(name, shape, dt=F32):
            return ctx.enter_context(nc.sbuf_tensor(name, shape, dt))

        def sem(name):
            return ctx.enter_context(nc.semaphore(name))

        w = sb("w", [P, W_ALL])
        vec = sb("vec", [P, V_ALL])
        cst = sb("cst", [P, C_ALL])
        brow = sb("brow", [P, E + D])
        bhi = sb("bhi", [P, E + D], BF16)
        bmid = sb("bmid", [P, E + D], BF16)
        brest = sb("brest", [P, E + D])
        brest2 = sb("brest2", [P, E + D])
        bsum = sb("bsum", [P, E + D])
        bsum2 = sb("bsum2", [P, E + D])
        bv3 = sb("bv3", [P, 2, E], BF16)
        bo3 = sb("bo3", [P, NT, D], BF16)
        ones = sb("ones", [P, P], BF16)
        ln2w = sb("ln2w", [P, D])
        ln2b = sb("ln2b", [P, D])
        pos = sb("pos", [2 * MAX_REL + 1, 1])
        posb = sb("posb", [2 * MAX_REL + 1, GROUP])
        biasrow = sb("biasrow", [GROUP, P])
        bias = sb("bias", [P, GROUP])
        heads = sb("heads", [P, 4 * QK])
        mhalf = sb("mhalf", [P, 2, NT])
        table = sb("table", [P, 1])
        wf = sb("wf", [P, D])
        wn = sb("wn", [P, W_O])
        whi = sb("whi", [P, W_O], F32R)
        wlo = sb("wlo", [P, W_O], F32R)
        ln1b_wide = sb("ln1b_wide", [P, P])
        pbias = sb("pbias", [P, EC + 1])

        X = [sb(f"X{p}", [P, NT, D]) for p in range(2)]
        st = sb("st", [P, NT, 6])
        mv = sb("mv", [P, NT, 2])
        var = sb("var", [P, 2, NT])
        rstd = sb("rstd", [P, 2, NT])
        shift1 = sb("shift1", [P, NT])
        xn = sb("xn", [P, NT, D])
        xa = sb("xa", [P, NT, D])
        xnT = sb("xnT", [P, NB, SEQ + 1])
        xhi = sb("xhi", [P, UNIT], F32R)
        xlo = sb("xlo", [P, UNIT], F32R)
        step = sb("step", [P, NB, SEQ])
        xr = sb("xr", [P, NB, SEQ])
        xk = sb("xk", [P, NB, SEQ])
        kr = sb("kr", [P, UNIT])
        kact = sb("kact", [P, UNIT])
        rt = sb("rt", [P, UNIT])
        ffn = sb("ffn", [P, UNIT])
        xb = sb("xb", [P, NT, D])
        rest = sb("rest", [P, UNIT])
        s = sb("s", [2 * QK, UNIT])
        Z = sb("Z", [P, NB, SEQ])
        hd = sb("hd", [P, UNIT])
        k = sb("k", [2 * QK, UNIT])
        lk = sb("lk", [P, NT, QK])
        v = sb("v", [P, NT, E])
        g = [sb(f"g{p}", [P, EC, UNIT]) for p in range(2)]
        a1 = sb("a1", [P, NT, GROUP])
        a2 = sb("a2", [P, NT, P])
        kvs = sb("kvs", [3 * QK, NB, E], F32R)
        lqs = sb("lqs", [3 * QK, UNIT], F32R)
        gated = sb("gated", [P, EC, UNIT])
        st2 = sb("st2", [P, NT, 6])
        mv2 = sb("mv2", [P, NT, 2])
        var3 = sb("var3", [P, NT])
        rstd3 = sb("rstd3", [P, NT])
        o1 = sb("o1", [P, NT, D])
        Y = sb("Y", [P, NT, D])

        ps = ctx.enter_context(nc.psum_tensor("ps", [P, 8, 512], F32))
        ident = cst[:, C_ID:C_ID + P]
        rope = cst[:, C_ROPE:C_ROPE + SEQ]
        p_lk = p_kv = p_qk = ps[:, 0, :]
        p_heads = p_k = ps[:, 1, :]
        p_r = p_o = ps[:, 2, :]
        p_att = p_v = ps[:, 3:5, :]
        p_scores = p_ffn = ps[:, 5, :]
        p_xn, p_xa = ps[:, 6, :], ps[:, 7, :]
        p_posrow = ps[0:GROUP, 3, 0:P]
        p_g = ps[:, 6:8, :]

        w_loaded, vec_loaded, cst_loaded = sem("w_loaded"), sem("vec_loaded"), sem("cst_loaded")
        brow_loaded, ln2_loaded, pos_loaded = sem("brow_loaded"), sem("ln2_loaded"), sem("pos_loaded")
        biasrow_stored, bias_loaded = sem("biasrow_stored"), sem("bias_loaded")
        x_loaded = [sem(f"x_loaded{p}") for p in range(2)]
        y_stored = sem("y_stored")
        setup_dve, setup_pe, setup_pool = sem("setup_dve"), sem("setup_pe"), sem("setup_pool")
        split_step, posrow_ready, heads_built = sem("split_step"), sem("posrow_ready"), sem("heads_built")
        w_split, pbias_done, pbias_ready = sem("w_split"), sem("pbias_done"), sem("pbias_ready")
        stats_ready, aggr_ready, var_ready = sem("stats_ready"), sem("aggr_ready"), sem("var_ready")
        rstd_ready, shift1_ready = sem("rstd_ready"), sem("shift1_ready")
        xa_ready, xn_ready, xT_done = sem("xa_ready"), sem("xn_ready"), sem("xT_done")
        xaT_done = sem("xaT_done")
        xhi_ready, xlo_ready, xnT_ready = sem("xhi_ready"), sem("xlo_ready"), sem("xnT_ready")
        step_ready, mix_ready = sem("step_ready"), sem("mix_ready")
        qk_done, s_ready, Z_ready = sem("qk_done"), sem("s_ready"), sem("Z_ready")
        heads_done, lk_done = sem("heads_done"), sem("lk_done")
        heads_ready, lk_ready = sem("heads_ready"), sem("lk_ready")
        g_done, g_ready, v_done, v_ready = sem("g_done"), sem("g_ready"), sem("v_done"), sem("v_ready")
        scores_done, a1_ready, a2_ready = sem("scores_done"), sem("a1_ready"), sem("a2_ready")
        k_done, kr_ready, kact_ready = sem("k_done"), sem("kr_ready"), sem("kact_ready")
        r_done, rt_ready = sem("r_done"), sem("rt_ready")
        ffnv_done, ffn_ready, xb_ready, rest_ready = (
            sem("ffnv_done"), sem("ffn_ready"), sem("xb_ready"), sem("rest_ready"))
        kv_done, kvh_ready, kv_ready = sem("kv_done"), sem("kvh_ready"), sem("kv_ready")
        lq_ready = sem("lq_ready")
        att_done, gated_ready, o_done = sem("att_done"), sem("gated_ready"), sem("o_done")
        stats3_ready, aggr3_ready, var3_ready, rstd3_ready, o1_ready, y_ready = (
            sem("stats3_ready"), sem("aggr3_ready"), sem("var3_ready"), sem("rstd3_ready"),
            sem("o1_ready"), sem("y_ready"))

        block = ctx.enter_context(nc.Block())

        def later(u):
            return not isinstance(u, int) or u > 0

        def pipeline(eng, first, slot, last=None):
            first()
            slot(0, 0, True)
            with eng.Fori(0, units // 2 - 1) as j:
                slot(j, 1, True)
                slot(j + 1, 0, True)
            slot(units // 2 - 1, 1, False)
            if last:
                last()

        def following(i, p):
            return (i, 1) if p == 0 else (i + 1, 0)

        @block.sync
        def _(sp):
            sp.dma_start(X[0][:], x_units[0]).then_inc(x_loaded[0], 16)
            sp.dma_start(w[:], weights).then_inc(w_loaded, 16)
            sp.dma_start(X[1][:], x_units[1]).then_inc(x_loaded[1], 16)
            sp.wait_ge(posrow_ready, 1)
            sp.dma_start(scratch, biasrow[:]).then_inc(biasrow_stored, 16)
            sp.wait_ge(biasrow_stored, 16)
            skewed = bass.AP(scratch.tensor, GROUP - 1, [[P - 1, GROUP], [1, GROUP]])
            for h in range(HG):
                sp.dma_start(bias[h * GROUP:(h + 1) * GROUP, :], skewed).then_inc(bias_loaded, 16)

            def slot(i, p, load):
                u = i * 2 + p
                if load:
                    sp.wait_ge(xa_ready, u + 1)
                    sp.wait_ge(xn_ready, u + 1)
                    sp.wait_ge(xb_ready, u + 1)
                    sp.dma_start(X[p][:], x_units[u + 2]).then_inc(x_loaded[p], 16)
                sp.wait_ge(y_ready, NT * (u + 1))
                sp.dma_start(out_units[u], Y[:]).then_inc(y_stored, 16)

            slot(0, 0, True)
            with sp.Fori(0, units // 2 - 2) as j:
                slot(j, 1, True)
                slot(j + 1, 0, True)
            slot(units // 2 - 2, 1, True)
            slot(units // 2 - 1, 0, False)
            slot(units // 2 - 1, 1, False)
            sp.wait_ge(y_stored, 16 * units)

        @block.gpsimd
        def _(pool):
            pool.memset(mhalf[:], -0.5).then_inc(setup_pool, 1)
            pool.memset(ones[:], 1.0).then_inc(setup_pool, 1)
            for b in range(NB):
                pool.memset(xnT[:, b, 0:1], 0.0).then_inc(setup_pool, 1)
            pool.memset(a2[:], 0.0).then_inc(setup_pool, 1)
            pool.wait_ge(setup_pool, 3 + NB)

            def rstds(n):
                pool.wait_ge(var_ready, 2 * (n + 1))
                if later(n):
                    pool.wait_ge(xa_ready, n)
                    pool.wait_ge(xn_ready, n)
                pool.tensor_tensor(rstd[:], var[:], mhalf[:], ALU.pow).then_inc(rstd_ready, 1)

            def first():
                rstds(0)
                pool.wait_ge(cst_loaded, 16)
                pool.wait_ge(vec_loaded, 16)
                for h in range(4):
                    pool.tensor_scalar(heads[:, h * QK:(h + 1) * QK], cst[:, C_HEADEYE:C_HEADEYE + QK],
                                       vec[:, V_HEADS + h:V_HEADS + h + 1], None, ALU.mult
                                       ).then_inc(heads_built, 1)
                for b in range(NB):
                    pool.tensor_copy(Z[:, b, :], rope).then_inc(heads_built, 1)
                pool.wait_ge(heads_built, 4 + NB)

            def slot(i, p, more):
                u = i * 2 + p
                pool.wait_ge(xnT_ready, u + 1)
                if later(u):
                    pool.wait_ge(mix_ready, 2 * u)
                pool.tensor_tensor(step[:], xnT[:, :, 1:SEQ + 1], xnT[:, :, 0:SEQ],
                                   ALU.subtract).then_inc(step_ready, 1)
                pool.wait_ge(s_ready, u + 1)
                if later(u):
                    pool.wait_ge(heads_done, u)
                pool.tensor_tensor(Z[0:2 * QK, :, :], s[:].rearrange("p (b n) -> p b n", b=NB),
                                   rope[0:2 * QK, :].unsqueeze(1).to_broadcast([2 * QK, NB, SEQ]),
                                   ALU.mult).then_inc(Z_ready, 1)
                if more:
                    rstds(u + 1)
                pool.wait_ge(rstd_ready, u + 2 if more else u + 1)
                pool.wait_ge(Z_ready, u + 1)
                pool.wait_ge(heads_ready, 4 * (u + 1))
                pool.tensor_tensor(lqs[QK:2 * QK, :], hd[0:QK, :], lqs[0:QK, :].bitcast(F32),
                                   ALU.subtract).then_inc(lq_ready, 1)
                pool.wait_ge(lq_ready, u + 1)
                pool.wait_ge(ln2_loaded, 32)
                pool.wait_ge(x_loaded[p], 16 * (i + 1))
                if later(u):
                    pool.wait_ge(rest_ready, u)
                pool.tensor_tensor(xb[:], X[p][:], ln2b[:].unsqueeze(1).to_broadcast([P, NT, D]),
                                   ALU.add).then_inc(xb_ready, 1)
                if later(u):
                    rstd3s(u - 1)
                pool.wait_ge(kr_ready, u + 1)
                if later(u):
                    pool.wait_ge(ffnv_done, u)
                pool.tensor_tensor(kact[:], kr[:], kr[:], ALU.mult).then_inc(kact_ready, 1)
                pool.wait_ge(ffn_ready, u + 1)
                pool.wait_ge(xb_ready, u + 1)
                if later(u):
                    pool.wait_ge(y_ready, NT * u)
                pool.tensor_tensor(rest[:], ffn[:], xb[:].rearrange("p t d -> p (t d)"),
                                   ALU.add).then_inc(rest_ready, 1)

            def rstd3s(n):
                pool.wait_ge(var3_ready, n + 1)
                if later(n):
                    pool.wait_ge(y_ready, NT * n)
                pool.tensor_tensor(rstd3[:], var3[:], mhalf[:, 0, :], ALU.pow).then_inc(rstd3_ready, 1)

            def last():
                rstd3s(units - 1)

            pipeline(pool, first, slot, last)

        @block.vector
        def _(dve):
            def put(ins, n):
                ins.then_inc(split_step, 1)
                dve.wait_ge(split_step, n)

            def split_weights():
                dve.wait_ge(w_loaded, 16)
                dve.tensor_scalar(wn[:], w[:, 0:W_O], vec[:, V_LN1W:V_LN1W + 1], None, ALU.mult
                                  ).then_inc(w_split, 1)
                dve.wait_ge(w_split, 1)
                dve.tensor_copy(whi[:], wn[:]).then_inc(w_split, 1)
                dve.wait_ge(w_split, 2)
                dve.tensor_tensor(wlo[:], wn[:], whi[:].bitcast(F32), ALU.subtract
                                  ).then_inc(w_split, 1)

            def column_biases():
                dve.wait_ge(pbias_done, 2)
                dve.tensor_tensor(pbias[:], vec[:, V_BG:V_BG + EC + 1], p_scores[:, E:E + EC + 1],
                                  ALU.add).then_inc(pbias_ready, 1)

            def row_biases():
                dve.wait_ge(brow_loaded, 32)
                put(dve.tensor_tensor(brow[:, 0:E], brow[:, 0:E], p_v[:, 1, 0:E], ALU.add), 1)
                put(dve.tensor_copy(bhi[:], brow[:]), 2)
                put(dve.tensor_tensor(brest[:], brow[:], bhi[:], ALU.subtract), 3)
                put(dve.tensor_copy(bmid[:], brest[:]), 4)
                put(dve.tensor_tensor(brest2[:], brest[:], bmid[:], ALU.subtract), 5)
                split = cst[:, C_SPLIT:C_SPLIT + 3]
                put(dve.tensor_scalar(bsum[:], bhi[:], split[:, 0:1], None, ALU.mult), 6)
                put(dve.scalar_tensor_tensor(out=bsum2[:], in0=bmid[:], scalar=split[:, 1:2],
                                             in1=bsum[:], op0=ALU.mult, op1=ALU.add), 7)
                put(dve.scalar_tensor_tensor(out=bsum[:], in0=brest2[:], scalar=split[:, 2:3],
                                             in1=bsum2[:], op0=ALU.mult, op1=ALU.add), 8)
                dve.tensor_copy(bv3[:], bsum[:, 0:E].unsqueeze(1).to_broadcast([P, 2, E])
                                ).then_inc(setup_dve, 1)
                dve.tensor_copy(bo3[:], bsum[:, E:E + D].unsqueeze(1).to_broadcast([P, NT, D])
                                ).then_inc(setup_dve, 1)
                dve.tensor_scalar(wf[:], w[:, W_F:W_F + D], 0.5, None, ALU.mult).then_inc(setup_dve, 1)

            def wide_columns():
                dve.wait_ge(cst_loaded, 16)
                dve.wait_ge(vec_loaded, 16)
                dve.tensor_scalar(ln1b_wide[:], cst[:, C_ID:C_ID + P], 0.0,
                                  vec[:, V_LN1B:V_LN1B + 1], ALU.mult, ALU.add).then_inc(setup_dve, 1)
                dve.wait_ge(pos_loaded, 16)
                dve.tensor_scalar(posb[:], cst[0:2 * MAX_REL + 1, C_ID:C_ID + GROUP], 0.0,
                                  pos[:, 0:1], ALU.mult, ALU.add).then_inc(setup_dve, 1)

            def position_bias():
                dve.wait_ge(setup_pe, 1)
                dve.tensor_copy(biasrow[:], p_posrow).then_inc(posrow_ready, 1)

            def stats(i, p, n):
                dve.wait_ge(x_loaded[p], 16 * (i + 1))
                for t in range(NT):
                    dve.bn_stats(st[:, t, :], X[p][:, t, :]).then_inc(stats_ready, 1)

            def variances(n):
                for t in range(NT):
                    dve.bn_aggr(mv[:, t, :], st[:, t, :]).then_inc(aggr_ready, 1)
                dve.wait_ge(aggr_ready, NT * (n + 1))
                dve.tensor_scalar(var[:, 0, :], mv[:, :, 1], EPS, None, ALU.add
                                  ).then_inc(var_ready, 1)
                dve.tensor_scalar(var[:, 1, :], mv[:, :, 1], 1.0 + EPS, EPS * EPS, ALU.mult, ALU.add
                                  ).then_inc(var_ready, 1)

            def shift(n):
                dve.wait_ge(rstd_ready, n + 1)
                if later(n):
                    dve.wait_ge(xn_ready, n)
                dve.scalar_tensor_tensor(out=shift1[:], in0=mv[:, :, 0], scalar=-1.0,
                                         in1=rstd[:, 0, :], op0=ALU.mult, op1=ALU.mult
                                         ).then_inc(shift1_ready, 1)

            def norm_twice(p, n):
                dve.wait_ge(rstd_ready, n + 1)
                if later(n):
                    dve.wait_ge(xaT_done, n)
                for t in range(NT):
                    last = dve.tensor_scalar(xa[:, t, :], X[p][:, t, :], mv[:, t, 0:1],
                                             rstd[:, 1, t:t + 1], ALU.subtract, ALU.mult)
                last.then_inc(xa_ready, 1)

            def low_part(n):
                dve.wait_ge(xhi_ready, n + 1)
                if later(n):
                    dve.wait_ge(v_done, 2 * n)
                dve.tensor_tensor(xlo[:], p_xa, xhi[:].bitcast(F32), ALU.subtract
                                  ).then_inc(xlo_ready, 1)

            def mix(dst, mu):
                dve.scalar_tensor_tensor(out=dst[:], in0=step[:], scalar=vec[:, mu:mu + 1],
                                         in1=xnT[:, :, 0:SEQ], op0=ALU.mult, op1=ALU.add
                                         ).then_inc(mix_ready, 1)

            def linear_keys(n):
                dve.wait_ge(lk_done, n + 1)
                if later(n):
                    dve.wait_ge(kv_done, n)
                dve.tensor_copy(lk[:].rearrange("p t d -> p (t d)"), p_lk[:, 0:NT * QK]
                                ).then_inc(lk_ready, 1)

            def low_kv(n):
                for b in range(NB):
                    if later(n):
                        dve.wait_ge(att_done, EC * n)
                    dve.wait_ge(kvh_ready, NB * n + b + 1)
                    dve.scalar_tensor_tensor(out=kvs[2 * QK:3 * QK, b, :],
                                             in0=p_kv[2 * b * QK:(2 * b + 1) * QK, 0:E],
                                             scalar=1.0 / SEQ, in1=kvs[0:QK, b, :].bitcast(F32),
                                             op0=ALU.mult, op1=ALU.subtract).then_inc(kv_ready, 1)

            def gate(p, n):
                for c in range(EC):
                    dve.wait_ge(g_ready, EC * n + c + 1)
                    if later(n):
                        dve.wait_ge(o_done, n)
                    dve.wait_ge(att_done, EC * n + c + 1)
                    dve.tensor_tensor(gated[:, c, :], p_att[:, c, :], g[p][:, c, :], ALU.mult
                                      ).then_inc(gated_ready, 1)

            def out_norm(n):
                dve.wait_ge(o_done, n + 1)
                for t in range(NT):
                    dve.bn_stats(st2[:, t, :], p_o[:, t * D:(t + 1) * D]).then_inc(stats3_ready, 1)

            def out_variances(n):
                for t in range(NT):
                    dve.bn_aggr(mv2[:, t, :], st2[:, t, :]).then_inc(aggr3_ready, 1)
                dve.wait_ge(aggr3_ready, NT * (n + 1))
                dve.tensor_scalar(var3[:], mv2[:, :, 1], EPS, None, ALU.add).then_inc(var3_ready, 1)
                for t in range(NT):
                    dve.scalar_tensor_tensor(out=o1[:, t, :], in0=p_o[:, t * D:(t + 1) * D],
                                             scalar=mv2[:, t, 0:1], in1=ln2w[:],
                                             op0=ALU.subtract, op1=ALU.mult).then_inc(o1_ready, 1)

            def output(n):
                dve.wait_ge(o1_ready, NT * (n + 1))
                dve.wait_ge(rest_ready, n + 1)
                if later(n):
                    dve.wait_ge(y_stored, 16 * n)
                dve.wait_ge(rstd3_ready, n + 1)
                for t in range(NT):
                    dve.scalar_tensor_tensor(out=Y[:, t, :], in0=o1[:, t, :],
                                             scalar=rstd3[:, t:t + 1], in1=rest[:, t * D:(t + 1) * D],
                                             op0=ALU.mult, op1=ALU.add).then_inc(y_ready, 1)

            def first():
                stats(0, 0, 0)
                dve.wait_ge(stats_ready, NT)
                variances(0)
                wide_columns()
                norm_twice(0, 0)
                shift(0)
                split_weights()
                low_part(0)
                column_biases()
                position_bias()
                row_biases()

            def slot(i, p, more):
                u = i * 2 + p
                if later(u):
                    gate(1 - p, u - 1)
                if more:
                    ni, np_ = following(i, p)
                    stats(ni, np_, u + 1)
                if more:
                    dve.wait_ge(stats_ready, NT * (u + 2))
                if later(u):
                    dve.wait_ge(r_done, u)
                dve.wait_ge(step_ready, u + 1)
                mix(xk, V_MUK)
                if more:
                    variances(u + 1)
                if later(u):
                    dve.wait_ge(ln2_loaded, 32)
                    out_norm(u - 1)
                    dve.wait_ge(stats3_ready, NT * u)
                mix(xr, V_MUR)
                if later(u):
                    out_variances(u - 1)
                if more:
                    shift(u + 1)
                dve.wait_ge(bias_loaded, 32)
                dve.wait_ge(scores_done, u + 1)
                dve.scalar_tensor_tensor(out=a1[:], scalar=1.0 / GROUP,
                                         in0=p_scores[:, 0:NT * GROUP].rearrange(
                                             "p (t j) -> p t j", t=NT),
                                         in1=bias[:].unsqueeze(1).to_broadcast([P, NT, GROUP]),
                                         op0=ALU.mult, op1=ALU.add).then_inc(a1_ready, 1)
                linear_keys(u)
                if later(u):
                    dve.wait_ge(att_done, EC * u)
                dve.wait_ge(a1_ready, u + 1)
                for h in range(HG):
                    at = slice(h * GROUP, (h + 1) * GROUP)
                    dve.scalar_tensor_tensor(out=a2[at, :, at], in0=a1[at, :, :], scalar=0.0,
                                             in1=a1[at, :, :], op0=ALU.max, op1=ALU.mult
                                             ).then_inc(a2_ready, 1)
                if more:
                    norm_twice(np_, u + 1)
                if later(u):
                    output(u - 1)
                if more:
                    low_part(u + 1)
                low_kv(u)
                dve.wait_ge(rt_ready, u + 1)
                if later(u):
                    dve.wait_ge(rest_ready, u)
                dve.wait_ge(ffnv_done, u + 1)
                dve.scalar_tensor_tensor(out=ffn[:], in0=rt[:], scalar=1.0, in1=p_ffn,
                                         op0=ALU.add, op1=ALU.mult).then_inc(ffn_ready, 1)

            def last():
                n = units - 1
                gate(n % 2, n)
                out_norm(n)
                dve.wait_ge(stats3_ready, NT * units)
                out_variances(n)
                output(n)

            pipeline(dve, first, slot, last)

        @block.scalar
        def _(act):
            act.dma_start(cst[:], consts).then_inc(cst_loaded, 16)
            act.dma_start(vec[:], vectors).then_inc(vec_loaded, 16)
            act.dma_start(pos[:], pos_emb.unsqueeze(1)).then_inc(pos_loaded, 16)
            act.dma_start(brow[:, 0:E], bv.unsqueeze(0).to_broadcast([P, E])).then_inc(brow_loaded, 16)
            act.dma_start(brow[:, E:E + D], bo.unsqueeze(0).to_broadcast([P, D])).then_inc(brow_loaded, 16)
            act.dma_start(ln2w[:], ln2_w.unsqueeze(0).to_broadcast([P, D])).then_inc(ln2_loaded, 16)
            act.dma_start(ln2b[:], ln2_b.unsqueeze(0).to_broadcast([P, D])).then_inc(ln2_loaded, 16)

            act.wait_ge(setup_pool, 1)
            act.activation(table[:], mhalf[:, 0, 0:1], ACT.Silu)

            def norm(p, n):
                act.wait_ge(shift1_ready, n + 1)
                if later(n):
                    act.wait_ge(xT_done, n)
                for t in range(NT):
                    last = act.activation(xn[:, t, :], X[p][:, t, :], ACT.Identity,
                                          bias=shift1[:, t:t + 1], scale=rstd[:, 0, t:t + 1])
                last.then_inc(xn_ready, 1)

            def high_part(n):
                if later(n):
                    act.wait_ge(v_done, 2 * n)
                act.wait_ge(xaT_done, n + 1)
                act.activation(xhi[:], p_xa, ACT.Identity).then_inc(xhi_ready, 1)

            def transposed(n):
                if later(n):
                    act.wait_ge(mix_ready, 2 * n)
                act.wait_ge(xT_done, n + 1)
                act.activation(xnT[:, :, 1:SEQ + 1], p_xn.rearrange("p (b n) -> p b n", b=NB),
                               ACT.Identity).then_inc(xnT_ready, 1)

            def silu_qk(n):
                act.wait_ge(qk_done, n + 1)
                if later(n):
                    act.wait_ge(Z_ready, n)
                act.activation(s[:], p_qk[0:2 * QK, :], ACT.Silu, bias=pbias[0:2 * QK, EC:EC + 1]
                               ).then_inc(s_ready, 1)

            def silu_gate(p, n):
                for c in range(EC):
                    act.wait_ge(g_done, EC * n + c + 1)
                    if c == 0 and later(n) and later(n - 1):
                        act.wait_ge(gated_ready, EC * (n - 1))
                    act.activation(g[p][:, c, :], p_g[:, c, :], ACT.Silu, bias=pbias[:, c:c + 1]
                                   ).then_inc(g_ready, 1)

            def move_heads(n):
                act.wait_ge(heads_done, n + 1)
                if later(n):
                    act.wait_ge(att_done, EC * n)
                act.activation(hd[:], p_heads, ACT.Identity).then_inc(heads_ready, 1)
                act.activation(k[QK:2 * QK, :], p_heads[2 * QK:3 * QK, :], ACT.Identity).then_inc(heads_ready, 1)
                for r in (0, 2):
                    act.activation(lqs[r * QK:(r + 1) * QK, :], p_heads[0:QK, :], ACT.Identity
                                   ).then_inc(heads_ready, 1)

            def silu_values(n):
                for h in range(2):
                    act.wait_ge(v_done, 2 * n + h + 1)
                    if later(n):
                        act.wait_ge(att_done, 2 * n)
                    act.activation(v[:, 2 * h:2 * h + 2, :].rearrange("p t e -> p (t e)"),
                                   p_v[:, h, :], ACT.Silu).then_inc(v_ready, 1)

            def first():
                norm(0, 0)
                high_part(0)
                transposed(0)
                act.wait_ge(pbias_ready, 1)
                silu_qk(0)
                silu_gate(0, 0)
                move_heads(0)
                silu_values(0)

            def slot(i, p, more):
                u = i * 2 + p
                if more:
                    ni, np_ = following(i, p)
                    act.wait_ge(x_loaded[np_], 16 * (ni + 1))
                    norm(np_, u + 1)
                act.wait_ge(k_done, u + 1)
                if later(u):
                    act.wait_ge(kact_ready, u)
                act.activation(kr[:], p_k, ACT.Relu).then_inc(kr_ready, 1)
                act.wait_ge(r_done, u + 1)
                if later(u):
                    act.wait_ge(ffn_ready, u)
                act.activation(rt[:], p_r, ACT.Tanh, scale=0.5).then_inc(rt_ready, 1)
                act.wait_ge(kv_done, u + 1)
                if later(u):
                    act.wait_ge(att_done, EC * u)
                for b in range(NB):
                    act.activation(kvs[0:2 * QK, b, :], p_kv[2 * b * QK:2 * (b + 1) * QK, 0:E],
                                   ACT.Identity, scale=1.0 / SEQ).then_inc(kvh_ready, 1)
                if more:
                    high_part(u + 1)
                    transposed(u + 1)
                    silu_qk(u + 1)
                    silu_gate(1 - p, u + 1)
                    move_heads(u + 1)
                    silu_values(u + 1)

            pipeline(act, first, slot)

        @block.tensor
        def _(pe):
            pe.wait_ge(cst_loaded, 16)
            pe.wait_ge(setup_dve, 2)
            pe.matmul(p_posrow, posb[:], cst[0:2 * MAX_REL + 1, C_SEL:C_SEL + P],
                      start=True, stop=True).then_inc(setup_pe, 1)

            def ln1_biases():
                pe.wait_ge(w_loaded, 16)
                b = vec[:, V_LN1B:V_LN1B + 1]
                pe.matmul(p_v[:, 1, 0:E], ln1b_wide[:], w[:, W_V:W_V + E], start=True, stop=True
                          ).then_inc(pbias_done, 1)
                for c in range(EC):
                    pe.matmul(p_scores[:, E + c:E + c + 1], w[:, W_G + c * P:W_G + (c + 1) * P], b,
                              start=True, stop=True)
                pe.matmul(p_scores[:, E + EC:E + EC + 1], w[:, W_QK:W_QK + P], b,
                          start=True, stop=True).then_inc(pbias_done, 1)

            def tile(t):
                return slice(t * P, (t + 1) * P)

            def transposes_xa(n):
                if later(n):
                    pe.wait_ge(g_ready, EC * n)
                pe.wait_ge(xa_ready, n + 1)
                for t in range(NT):
                    last = pe.transpose(p_xa[:, tile(t)], xa[:, t, :], ident)
                last.then_inc(xaT_done, 1)

            def transposes_xn(n):
                pe.wait_ge(xn_ready, n + 1)
                for t in range(NT):
                    last = pe.transpose(p_xn[:, tile(t)], xn[:, t, :], ident)
                last.then_inc(xT_done, 1)

            def project(dst, at):
                pe.matmul(dst, whi[:, at:at + P], xhi[:], start=True, stop=False)
                pe.matmul(dst, wlo[:, at:at + P], xhi[:], start=False, stop=False)
                return pe.matmul(dst, whi[:, at:at + P], xlo[:], start=False, stop=True)

            def project_qk(n):
                pe.wait_ge(xlo_ready, n + 1)
                if later(n):
                    pe.wait_ge(kv_ready, NB * n)
                project(p_qk, W_QK).then_inc(qk_done, 1)

            def project_gate(n):
                pe.wait_ge(xnT_ready, n + 1)
                for c in range(EC):
                    project(p_g[:, c, :], W_G + c * P).then_inc(g_done, 1)

            def rotary_heads(n):
                if later(n):
                    pe.wait_ge(kr_ready, n)
                pe.wait_ge(Z_ready, n + 1)
                pe.matmul(p_heads, heads[:], Z[:].rearrange("p b n -> p (b n)"), start=True, stop=True
                          ).then_inc(heads_done, 1)

            def project_values(n):
                if later(n):
                    pe.wait_ge(gated_ready, EC * n)
                wv = slice(W_V, W_V + E)
                for h in range(2):
                    pe.matmul(p_v[:, h, :], ones[:], bv3[:].rearrange("p a e -> p (a e)"),
                              start=True, stop=False, skip_group_check=True)
                    for t in range(2):
                        x = tile(2 * h + t)
                        dst = p_v[:, h, t * E:(t + 1) * E]
                        pe.matmul(dst, xhi[:, x], whi[:, wv], start=False, stop=False,
                                  skip_group_check=True)
                        pe.matmul(dst, xhi[:, x], wlo[:, wv], start=False, stop=False,
                                  skip_group_check=True)
                        last = pe.matmul(dst, xlo[:, x], whi[:, wv], start=False, stop=True,
                                         skip_group_check=True)
                    last.then_inc(v_done, 1)

            def linear_keys(n):
                for t in range(NT):
                    last = pe.transpose(p_lk[:, t * QK:(t + 1) * QK], hd[3 * QK:P, tile(t)],
                                        cst[3 * QK:P, C_ID + 3 * QK:C_ID + P])
                last.then_inc(lk_done, 1)

            def first():
                transposes_xa(0)
                ln1_biases()
                transposes_xn(0)
                pe.wait_ge(w_split, 3)
                project_qk(0)
                project_gate(0)
                pe.wait_ge(heads_built, 4 + NB)
                rotary_heads(0)
                pe.wait_ge(setup_pool, 3 + NB)
                pe.wait_ge(setup_dve, 5)
                project_values(0)

            def slot(i, p, more):
                u = i * 2 + p
                if later(u):
                    pe.wait_ge(ffn_ready, u)
                pe.wait_ge(heads_ready, 4 * u + 2)
                for t in range(NT):
                    for h in range(HG):
                        x = slice(t * P + h * GROUP, t * P + (h + 1) * GROUP)
                        last = pe.matmul(p_scores[h * GROUP:(h + 1) * GROUP,
                                                  t * GROUP:(t + 1) * GROUP],
                                         k[QK:2 * QK, x], hd[QK:2 * QK, x], start=True, stop=True)
                last.then_inc(scores_done, 1)
                linear_keys(u)
                pe.wait_ge(heads_ready, 4 * (u + 1))
                pe.wait_ge(mix_ready, 2 * (u + 1))
                pe.matmul(p_k, w[:, W_K:W_K + D], xk[:].rearrange("p b n -> p (b n)"),
                          start=True, stop=True).then_inc(k_done, 1)
                if later(u):
                    pe.wait_ge(o1_ready, NT * u)
                for t in range(NT):
                    last = pe.matmul(p_r[:, tile(t)], xr[:].rearrange("p b n -> p (b n)")[:, tile(t)],
                                     w[:, W_R:W_R + D], start=True, stop=True)
                last.then_inc(r_done, 1)
                pe.wait_ge(v_ready, 2 * (u + 1))
                pe.wait_ge(lk_ready, u + 1)
                for t in range(2):
                    for b in range(NB):
                        for r in (2 * b, 2 * b + 1):
                            last = pe.matmul(p_kv[r * QK:(r + 1) * QK, 0:E], lk[:, 2 * b + t, :],
                                             v[:, 2 * b + t, :], start=(t == 0), stop=(t == 1))
                last.then_inc(kv_done, 1)
                if more:
                    transposes_xa(u + 1)
                pe.wait_ge(a2_ready, HG * (u + 1))
                for c in range(EC):
                    for t in range(NT):
                        pe.matmul(p_att[:, c, tile(t)], v[:, t, c * P:(c + 1) * P], a2[:, t, :],
                                  start=(t == 0), stop=False, skip_group_check=True)
                pe.wait_ge(kact_ready, u + 1)
                for t in range(NT):
                    last = pe.matmul(p_ffn[:, tile(t)], kact[:, tile(t)], wf[:],
                                     start=True, stop=True)
                last.then_inc(ffnv_done, 1)
                if more:
                    transposes_xn(u + 1)
                    project_qk(u + 1)
                pe.wait_ge(lq_ready, u + 1)
                pe.wait_ge(kv_ready, NB * (u + 1))
                for c in range(EC):
                    for b in range(NB):
                        last = pe.matmul(p_att[:, c, b * SEQ:(b + 1) * SEQ],
                                         kvs[:, b, c * P:(c + 1) * P],
                                         lqs[:, b * SEQ:(b + 1) * SEQ],
                                         start=False, stop=True, skip_group_check=True)
                    last.then_inc(att_done, 1)
                if more:
                    project_gate(u + 1)
                pe.wait_ge(rt_ready, u + 1)
                pe.matmul(p_o, ones[:], bo3[:].rearrange("p t d -> p (t d)"),
                          start=True, stop=False, skip_group_check=True)
                pe.wait_ge(gated_ready, EC * (u + 1))
                for t in range(NT):
                    for c in range(EC):
                        last = pe.matmul(p_o[:, tile(t)], gated[:, c, tile(t)],
                                         w[:, W_O + c * D:W_O + (c + 1) * D], start=False,
                                         stop=(c == EC - 1), skip_group_check=True)
                last.then_inc(o_done, 1)
                if more:
                    rotary_heads(u + 1)
                    project_values(u + 1)

            pipeline(pe, first, slot)


def constants():
    import numpy as np
    half = QK // 2
    c = np.zeros((P, C_ALL), np.float32)
    c[:, C_ID:C_ID + P] = np.eye(P)
    inv = np.float32(10000.0) ** (-np.arange(half, dtype=np.float32) / np.float32(half))
    angle = np.arange(SEQ, dtype=np.float32)[None, :] * inv.astype(np.float32)[:, None]
    cos, sin = np.cos(angle.astype(np.float64)), np.sin(angle.astype(np.float64))
    table = np.concatenate([cos, cos, -sin, sin])
    c[:, C_ROPE:C_ROPE + SEQ] = np.concatenate([table, table])
    c[:, C_HEADEYE:C_HEADEYE + QK] = np.tile(np.eye(QK), (4, 1))
    away = np.minimum(np.abs(np.arange(P) - (GROUP - 1)), MAX_REL)
    c[:, C_SEL:C_SEL + P] = np.arange(P)[:, None] == away[None, :]
    c[0:3, C_SPLIT:C_SPLIT + 3] = np.eye(3)
    return c


def kernel(L0_attn_x, L0_attn_ln1_w, L0_attn_ln1_b, L0_attn_Wqk, L0_attn_bqk, L0_attn_Wv, L0_attn_bv,
           L0_attn_Wg, L0_attn_bg, L0_attn_Wo, L0_attn_bo, L0_attn_ln2_w, L0_attn_ln2_b, L0_attn_gamma,
           L0_attn_beta, L0_attn_pos_emb, L0_ffn_W_r, L0_ffn_W_k, L0_ffn_W_v, L0_ffn_mu_r, L0_ffn_mu_k):
    import numpy as np
    import concourse.bacc as bacc
    from concourse.bass_utils import run_bass_kernel_spmd

    x = np.ascontiguousarray(L0_attn_x)
    half = QK // 2
    swap = np.r_[half:QK, 0:half]
    wo = np.asarray(L0_attn_Wo).T
    weights = np.concatenate(
        [L0_attn_Wqk.T, np.asarray(L0_attn_Wqk)[swap].T, L0_attn_Wv.T, L0_attn_Wg.T, wo[:P], wo[P:],
         L0_ffn_W_r.T, L0_ffn_W_k.T, L0_ffn_W_v.T], axis=1)
    vectors = np.zeros((P, V_ALL), np.float32)
    vectors[:, V_LN1W] = L0_attn_ln1_w
    vectors[:, V_LN1B] = L0_attn_ln1_b
    vectors[:, V_MUR] = L0_ffn_mu_r
    vectors[:, V_MUK] = L0_ffn_mu_k
    vectors[:, V_BG:V_BG + EC] = np.asarray(L0_attn_bg).reshape(EC, P).T
    bqk, gamma, beta = np.asarray(L0_attn_bqk), np.asarray(L0_attn_gamma), np.asarray(L0_attn_beta)
    vectors[0:2 * QK, V_BQK] = np.concatenate([bqk, bqk[swap]])
    heads = np.concatenate([gamma.T, gamma.T[swap], beta.T, beta.T[swap]])
    vectors[:, V_HEADS:V_HEADS + 4] = heads[:, [1, 0, 2, 3]]

    ins = {
        "x": x, "weights": np.ascontiguousarray(weights), "vectors": vectors,
        "bv": np.ascontiguousarray(L0_attn_bv), "bo": np.ascontiguousarray(L0_attn_bo),
        "ln2_w": np.ascontiguousarray(L0_attn_ln2_w), "ln2_b": np.ascontiguousarray(L0_attn_ln2_b),
        "pos_emb": np.ascontiguousarray(L0_attn_pos_emb), "consts": constants(),
    }
    nc = bacc.Bacc("TRN2", target_bir_lowering=False, num_devices=1)
    args = {name: nc.dram_tensor(f"in_{name}", a.shape, mybir.dt.from_np(a.dtype),
                                 kind="ExternalInput").ap() for name, a in ins.items()}
    out = nc.dram_tensor("out_y", x.shape, F32, kind="ExternalOutput").ap()
    block_kernel(nc, out=out, **args)
    r = run_bass_kernel_spmd(nc, [{f"in_{name}": a for name, a in ins.items()}], core_ids=[0])
    return r.results[0]["out_y"]
```

```python
from contextlib import ExitStack

import concourse.bass as bass
from concourse import mybir

ALU = mybir.AluOpType
ACT = mybir.ActivationFunctionType
F32 = mybir.dt.float32
BF16 = mybir.dt.bfloat16
F32R = mybir.dt.float32r

P = 128
SEQ = 256
D = 128
QK = 32
E = 256
EC = E // P
GROUP = 64
HG = P // GROUP
UNIT = 512
NB = UNIT // SEQ
NT = UNIT // P
MAX_REL = 32
WARM = 14
EPS = 1e-5

W_QK, W_V, W_G, W_O, W_R, W_K, W_F = 0, 64, 320, 576, 832, 960, 1088
W_ALL = 1216
V_LN1W, V_LN1B, V_MUR, V_MUK, V_BG, V_BQK, V_HEADS = 0, 1, 2, 3, 4, 6, 7
V_POS = 11
V_ALL = 12
R_BV, R_BO, R_LN2W, R_LN2B = 0, 256, 384, 512
R_ALL = 640
C_ID, C_ROPE, C_HEADEYE, C_SEL = 0, 128, 384, 416
C_ALL = 544


def block_kernel(nc, x, weights, vectors, rows, consts, out):
    tokens = x.shape[0] * x.shape[1]
    units = tokens // UNIT
    assert x.shape[1] == SEQ and tokens % UNIT == 0 and units % 2 == 0 and units >= 4
    x_units = x.rearrange("(u b) (t p) d -> u p (b t) d", b=NB, p=P)
    out_units = out.rearrange("(u b) (t p) d -> u p (b t) d", b=NB, p=P)
    scratch = nc.dram_tensor("bias_rows", (GROUP, P), F32, kind="Internal").ap()

    with ExitStack() as ctx:
        def sb(name, shape, dt=F32):
            return ctx.enter_context(nc.sbuf_tensor(name, shape, dt))

        def sem(name):
            return ctx.enter_context(nc.semaphore(name))

        w = sb("w", [P, W_ALL])
        vec = sb("vec", [P, V_ALL])
        cst = sb("cst", [P, C_ALL])
        row = sb("row", [P, R_ALL])
        idle = sb("idle", [P, P], BF16)
        posb = sb("posb", [2 * MAX_REL + 1, GROUP])
        biasrow = sb("biasrow", [GROUP, P])
        bias = sb("bias", [P, GROUP])
        heads = sb("heads", [P, 4 * QK])
        mhalf = sb("mhalf", [P, 2, NT])
        table = sb("table", [P, 1])
        wf = sb("wf", [P, D])
        whi = sb("whi", [P, W_O], F32R)
        wlo = sb("wlo", [P, W_O], F32R)
        ln1b_wide = sb("ln1b_wide", [P, P])
        pbias = sb("pbias", [P, EC + 1])

        X = [sb(f"X{p}", [P, NT, D]) for p in range(2)]
        st = sb("st", [P, NT, 6])
        mv = sb("mv", [P, NT, 2])
        var = sb("var", [P, 2, NT])
        rstd = sb("rstd", [P, 2, NT])
        shift1 = sb("shift1", [P, NT])
        xn = sb("xn", [P, NT, D])
        xa = sb("xa", [P, NT, D])
        xnT = sb("xnT", [P, NB, SEQ + 1])
        xhi = sb("xhi", [P, UNIT], F32R)
        xlo = sb("xlo", [P, UNIT], F32R)
        step = sb("step", [P, NB, SEQ])
        xr = sb("xr", [P, NB, SEQ])
        xk = sb("xk", [P, NB, SEQ])
        kr = sb("kr", [P, UNIT])
        kact = sb("kact", [P, UNIT])
        rt = sb("rt", [P, UNIT])
        ffn = sb("ffn", [P, UNIT])
        xb = sb("xb", [P, NT, D])
        rest = sb("rest", [P, UNIT])
        s = sb("s", [2 * QK, UNIT])
        Z = sb("Z", [P, NB, SEQ])
        hd = sb("hd", [P, UNIT])
        k = sb("k", [2 * QK, UNIT])
        lk = sb("lk", [P, NT, QK])
        v = sb("v", [P, NT, E])
        g = [sb(f"g{p}", [P, EC, UNIT]) for p in range(2)]
        a1 = sb("a1", [P, NT, GROUP])
        a2 = sb("a2", [P, NT, P])
        kvs = sb("kvs", [3 * QK, NB, E], F32R)
        lqs = sb("lqs", [3 * QK, UNIT], F32R)
        gated = sb("gated", [P, EC, UNIT])
        st2 = sb("st2", [P, NT, 6])
        mv2 = sb("mv2", [P, NT, 2])
        var3 = sb("var3", [P, NT])
        rstd3 = sb("rstd3", [P, NT])
        o1 = sb("o1", [P, NT, D])
        Y = sb("Y", [P, NT, D])

        ps = ctx.enter_context(nc.psum_tensor("ps", [P, 8, 512], F32))
        ln2w, ln2b = row[:, R_LN2W:R_LN2W + D], row[:, R_LN2B:R_LN2B + D]
        ident = cst[:, C_ID:C_ID + P]
        rope = cst[:, C_ROPE:C_ROPE + SEQ]
        p_lk = p_kv = p_qk = ps[:, 0, :]
        p_heads = p_k = ps[:, 1, :]
        p_r = p_o = ps[:, 2, :]
        p_att = p_v = ps[:, 3:5, :]
        p_scores = p_ffn = ps[:, 5, :]
        p_xn, p_xa = ps[:, 6, :], ps[:, 7, :]
        p_posrow, p_column, p_row = ps[0:GROUP, 1, 0:P], ps[:, 5, 0:EC + 1], ps[:, 5, E:2 * E]
        p_g = ps[:, 6:8, :]
        HT = NT // 2
        p_last = [p_o, p_k]

        w_loaded, vec_loaded, cst_loaded = sem("w_loaded"), sem("vec_loaded"), sem("cst_loaded")
        row_loaded = sem("row_loaded")
        biasrow_stored, bias_loaded = sem("biasrow_stored"), sem("bias_loaded")
        x_loaded = [sem(f"x_loaded{p}") for p in range(2)]
        y_stored = sem("y_stored")
        w_rest_loaded, rope_loaded = sem("w_rest_loaded"), sem("rope_loaded")
        setup_pool, idle_ready, heads_built = sem("setup_pool"), sem("idle_ready"), sem("heads_built")
        posb_ready, posrow_done, posrow_ready = sem("posb_ready"), sem("posrow_done"), sem("posrow_ready")
        ln1b_ready, wf_ready = sem("ln1b_ready"), sem("wf_ready")
        w_split, pbias_done, pbias_ready = sem("w_split"), sem("pbias_done"), sem("pbias_ready")
        row_ready = sem("row_ready")
        vbias_ready, obias_ready = sem("vbias_ready"), sem("obias_ready")
        rstd_xa0_ready = sem("rstd_xa0_ready")
        stats_ready, aggr_ready, var_ready = sem("stats_ready"), sem("aggr_ready"), sem("var_ready")
        rstd_ready, shift1_ready = sem("rstd_ready"), sem("shift1_ready")
        xa_ready, xn_ready, xT_done = sem("xa_ready"), sem("xn_ready"), sem("xT_done")
        xaT_done = sem("xaT_done")
        xhi_ready, xlo_ready, xnT_ready = sem("xhi_ready"), sem("xlo_ready"), sem("xnT_ready")
        step_ready, mix_ready = sem("step_ready"), sem("mix_ready")
        qk_done, s_ready, Z_ready = sem("qk_done"), sem("s_ready"), sem("Z_ready")
        heads_done, lk_done = sem("heads_done"), sem("lk_done")
        heads_ready, lk_ready = sem("heads_ready"), sem("lk_ready")
        g_done, g_ready, v_done, v_ready = sem("g_done"), sem("g_ready"), sem("v_done"), sem("v_ready")
        scores_done, a1_ready, a2_ready = sem("scores_done"), sem("a1_ready"), sem("a2_ready")
        k_done, kr_ready, kact_ready = sem("k_done"), sem("kr_ready"), sem("kact_ready")
        r_done, rt_ready = sem("r_done"), sem("rt_ready")
        ffnv_done, ffn_ready, xb_ready, rest_ready = (
            sem("ffnv_done"), sem("ffn_ready"), sem("xb_ready"), sem("rest_ready"))
        kv_done, kvh_ready, kv_ready = sem("kv_done"), sem("kvh_ready"), sem("kv_ready")
        lq_ready, lq_copied = sem("lq_ready"), sem("lq_copied")
        att_done, gated_ready, o_done = sem("att_done"), sem("gated_ready"), sem("o_done")
        stats3_ready, aggr3_ready, var3_ready, rstd3_ready, o1_ready, y_ready = (
            sem("stats3_ready"), sem("aggr3_ready"), sem("var3_ready"), sem("rstd3_ready"),
            sem("o1_ready"), sem("y_ready"))

        block = ctx.enter_context(nc.Block())

        def later(u):
            return not isinstance(u, int) or u > 0

        def pipeline(eng, first, slot, last=None):
            first()
            slot(0, 0, True)
            with eng.Fori(0, units // 2 - 1) as j:
                slot(j, 1, True)
                slot(j + 1, 0, True)
            slot(units // 2 - 1, 1, False)
            if last:
                last()

        def following(i, p):
            return (i, 1) if p == 0 else (i + 1, 0)

        @block.sync
        def _(sp):
            sp.dma_start(X[0][:], x_units[0]).then_inc(x_loaded[0], 16)
            sp.dma_start(w[:, 0:W_O], weights[:, 0:W_O]).then_inc(w_loaded, 16)
            lower = consts[2 * QK:P, C_ROPE:C_ROPE + SEQ]
            sp.dma_start(Z[2 * QK:P, :, :], lower.unsqueeze(1).to_broadcast([P - 2 * QK, NB, SEQ])
                         ).then_inc(rope_loaded, 16)
            sp.dma_start(w[:, W_O:W_ALL], weights[:, W_O:W_ALL]).then_inc(w_rest_loaded, 16)
            sp.dma_start(X[1][:], x_units[1]).then_inc(x_loaded[1], 16)
            sp.wait_ge(posrow_ready, 1)
            sp.dma_start(scratch, biasrow[:]).then_inc(biasrow_stored, 16)
            sp.wait_ge(biasrow_stored, 16)
            skewed = bass.AP(scratch.tensor, GROUP - 1, [[P - 1, GROUP], [1, GROUP]])
            for h in range(HG):
                sp.dma_start(bias[h * GROUP:(h + 1) * GROUP, :], skewed).then_inc(bias_loaded, 16)

            def load(i, p):
                u = i * 2 + p
                sp.wait_ge(xa_ready, NT * (u + 1))
                sp.wait_ge(xn_ready, u + 1)
                sp.wait_ge(xb_ready, u + 1)
                sp.dma_start(X[p][:], x_units[u + 2]).then_inc(x_loaded[p], 16)

            def store(u):
                sp.wait_ge(y_ready, NT * (u + 1))
                sp.dma_start(out_units[u], Y[:]).then_inc(y_stored, 16)

            load(0, 0)
            with sp.Fori(0, units // 2 - 2) as j:
                load(j, 1)
                store(j * 2)
                load(j + 1, 0)
                store(j * 2 + 1)
            load(units // 2 - 2, 1)
            for u in range(units - 4, units - 1):
                store(u)
            for t in range(NT):
                sp.wait_ge(y_ready, NT * (units - 1) + t + 1)
                sp.dma_start(out_units[units - 1][:, t:t + 1, :], Y[:, t:t + 1, :]
                             ).then_inc(y_stored, 16)
            sp.wait_ge(y_stored, 16 * (units - 1 + NT))

        @block.gpsimd
        def _(pool):
            pool.memset(mhalf[:], -0.5).then_inc(setup_pool, 1)
            pool.memset(idle[:], 1.0).then_inc(idle_ready, 1)
            for b in range(NB):
                pool.memset(xnT[:, b, 0:1], 0.0).then_inc(setup_pool, 1)
            pool.memset(a2[:], 0.0).then_inc(setup_pool, 1)
            pool.wait_ge(idle_ready, 1)
            pool.wait_ge(setup_pool, 2 + NB)

            def rstds(n):
                pool.wait_ge(var_ready, 2 * (n + 1))
                if later(n):
                    pool.wait_ge(xa_ready, NT * n)
                    pool.wait_ge(xn_ready, n)
                pool.tensor_tensor(rstd[:], var[:], mhalf[:], ALU.pow).then_inc(rstd_ready, 1)

            def first():
                pool.wait_ge(var_ready, 2)
                pool.tensor_tensor(rstd[:, 1, :], var[:, 1, :], mhalf[:, 1, :], ALU.pow
                                   ).then_inc(rstd_xa0_ready, 1)
                pool.tensor_tensor(rstd[:, 0, :], var[:, 0, :], mhalf[:, 0, :], ALU.pow
                                   ).then_inc(rstd_ready, 1)
                pool.wait_ge(cst_loaded, 16)
                pool.wait_ge(vec_loaded, 16)
                for h in range(4):
                    pool.tensor_scalar(heads[:, h * QK:(h + 1) * QK], cst[:, C_HEADEYE:C_HEADEYE + QK],
                                       vec[:, V_HEADS + h:V_HEADS + h + 1], None, ALU.mult
                                       ).then_inc(heads_built, 1)
                pool.wait_ge(heads_built, 4)

            def slot(i, p, more):
                u = i * 2 + p
                pool.wait_ge(xnT_ready, u + 1)
                if later(u):
                    pool.wait_ge(mix_ready, 2 * u)
                pool.tensor_tensor(step[:], xnT[:, :, 1:SEQ + 1], xnT[:, :, 0:SEQ],
                                   ALU.subtract).then_inc(step_ready, 1)
                if later(u):
                    pool.wait_ge(s_ready, u + 1)
                    pool.wait_ge(heads_done, u)
                    pool.tensor_tensor(Z[0:2 * QK, :, :], s[:].rearrange("p (b n) -> p b n", b=NB),
                                       rope[0:2 * QK, :].unsqueeze(1).to_broadcast([2 * QK, NB, SEQ]),
                                       ALU.mult).then_inc(Z_ready, 1)
                    rests(u - 1)
                if more:
                    rstds(u + 1)
                pool.wait_ge(rstd_ready, u + 2 if more else u + 1)
                pool.wait_ge(Z_ready, u + 1)
                if later(u):
                    pool.wait_ge(rest_ready, u)
                pool.wait_ge(heads_ready, 3 * (u + 1))
                pool.tensor_tensor(lqs[QK:2 * QK, :], hd[0:QK, :], lqs[0:QK, :].bitcast(F32),
                                   ALU.subtract).then_inc(lq_ready, 1)
                pool.wait_ge(lq_ready, u + 1)
                pool.wait_ge(row_loaded, 16)
                pool.wait_ge(x_loaded[p], 16 * (i + 1))
                if later(u):
                    pool.wait_ge(rest_ready, u)
                pool.tensor_tensor(xb[:], X[p][:], ln2b.unsqueeze(1).to_broadcast([P, NT, D]),
                                   ALU.add).then_inc(xb_ready, 1)
                if later(u):
                    rstd3s(u - 1)
                pool.wait_ge(kr_ready, u + 1)
                if later(u):
                    pool.wait_ge(ffnv_done, u)
                pool.tensor_tensor(kact[:], kr[:], kr[:], ALU.mult).then_inc(kact_ready, 1)

            def rests(n):
                pool.wait_ge(ffn_ready, n + 1)
                pool.wait_ge(xb_ready, n + 1)
                if later(n):
                    pool.wait_ge(y_ready, NT * n)
                pool.tensor_tensor(rest[:], ffn[:], xb[:].rearrange("p t d -> p (t d)"),
                                   ALU.add).then_inc(rest_ready, 1)

            def rstd3s(n):
                pool.wait_ge(var3_ready, n + 1)
                if later(n):
                    pool.wait_ge(y_ready, NT * n)
                pool.tensor_tensor(rstd3[:], var3[:], mhalf[:, 0, :], ALU.pow).then_inc(rstd3_ready, 1)

            def last():
                rests(units - 1)
                for h in range(2):
                    half = slice(h * HT, (h + 1) * HT)
                    pool.wait_ge(var3_ready, units + h)
                    if h == 0:
                        pool.wait_ge(y_ready, NT * (units - 1))
                    pool.tensor_tensor(rstd3[:, half], var3[:, half], mhalf[:, 0, half], ALU.pow
                                       ).then_inc(rstd3_ready, 1)

            pipeline(pool, first, slot, last)

        @block.vector
        def _(dve):
            def split_weights():
                dve.wait_ge(w_split, 1)
                dve.scalar_tensor_tensor(out=wlo[:], in0=w[:, 0:W_O], scalar=vec[:, V_LN1W:V_LN1W + 1],
                                         in1=whi[:].bitcast(F32), op0=ALU.mult, op1=ALU.subtract
                                         ).then_inc(w_split, 1)

            def column_biases():
                dve.wait_ge(pbias_done, 1)
                dve.tensor_tensor(pbias[:], vec[:, V_BG:V_BG + EC + 1], p_column,
                                  ALU.add).then_inc(pbias_ready, 1)

            def row_biases():
                dve.wait_ge(row_loaded, 16)
                dve.tensor_tensor(row[:, R_BV:R_BV + E], row[:, R_BV:R_BV + E], p_row,
                                  ALU.add).then_inc(row_ready, 1)

            def wide_columns():
                dve.tensor_scalar(posb[:], cst[0:2 * MAX_REL + 1, C_ID:C_ID + GROUP], 0.0,
                                  vec[0:2 * MAX_REL + 1, V_POS:V_POS + 1], ALU.mult, ALU.add).then_inc(posb_ready, 1)
                dve.tensor_scalar(ln1b_wide[:], cst[:, C_ID:C_ID + P], 0.0,
                                  vec[:, V_LN1B:V_LN1B + 1], ALU.mult, ALU.add).then_inc(ln1b_ready, 1)

            def position_bias():
                dve.wait_ge(posrow_done, 1)
                dve.tensor_copy(biasrow[:], p_posrow).then_inc(posrow_ready, 1)

            def stats(i, p, n):
                dve.wait_ge(x_loaded[p], 16 * (i + 1))
                for t in range(NT):
                    dve.bn_stats(st[:, t, :], X[p][:, t, :]).then_inc(stats_ready, 1)

            def variances(n):
                for t in range(NT):
                    dve.bn_aggr(mv[:, t, :], st[:, t, :]).then_inc(aggr_ready, 1)
                dve.wait_ge(aggr_ready, NT * (n + 1))
                dve.tensor_scalar(var[:, 0, :], mv[:, :, 1], EPS, None, ALU.add
                                  ).then_inc(var_ready, 1)
                dve.tensor_scalar(var[:, 1, :], mv[:, :, 1], 1.0 + EPS, EPS * EPS, ALU.mult, ALU.add
                                  ).then_inc(var_ready, 1)

            def shift(n):
                dve.wait_ge(rstd_ready, n + 1)
                if later(n):
                    dve.wait_ge(xn_ready, n)
                dve.scalar_tensor_tensor(out=shift1[:], in0=mv[:, :, 0], scalar=-1.0,
                                         in1=rstd[:, 0, :], op0=ALU.mult, op1=ALU.mult
                                         ).then_inc(shift1_ready, 1)

            def norm_twice(p, n):
                if later(n):
                    dve.wait_ge(rstd_ready, n + 1)
                    dve.wait_ge(xaT_done, n)
                for t in range(NT):
                    dve.tensor_scalar(xa[:, t, :], X[p][:, t, :], mv[:, t, 0:1],
                                      rstd[:, 1, t:t + 1], ALU.subtract, ALU.mult
                                      ).then_inc(xa_ready, 1)

            def low_part(n):
                dve.wait_ge(xhi_ready, n + 1)
                if later(n):
                    dve.wait_ge(v_done, 2 * n)
                dve.tensor_tensor(xlo[:], p_xa, xhi[:].bitcast(F32), ALU.subtract
                                  ).then_inc(xlo_ready, 1)

            def mix(dst, mu):
                dve.scalar_tensor_tensor(out=dst[:], in0=step[:], scalar=vec[:, mu:mu + 1],
                                         in1=xnT[:, :, 0:SEQ], op0=ALU.mult, op1=ALU.add
                                         ).then_inc(mix_ready, 1)

            def linear_keys(n):
                dve.wait_ge(lk_done, n + 1)
                if later(n):
                    dve.wait_ge(kv_done, n)
                dve.tensor_copy(lk[:].rearrange("p t d -> p (t d)"), p_lk[:, 0:NT * QK]
                                ).then_inc(lk_ready, 1)

            def low_kv(n):
                for b in range(NB):
                    if later(n):
                        dve.wait_ge(att_done, EC * n)
                    dve.wait_ge(kvh_ready, NB * n + b + 1)
                    dve.scalar_tensor_tensor(out=kvs[2 * QK:3 * QK, b, :],
                                             in0=p_kv[2 * b * QK:(2 * b + 1) * QK, 0:E],
                                             scalar=1.0 / SEQ, in1=kvs[0:QK, b, :].bitcast(F32),
                                             op0=ALU.mult, op1=ALU.subtract).then_inc(kv_ready, 1)

            def gate(p, n):
                for c in range(EC):
                    dve.wait_ge(g_ready, EC * n + c + 1)
                    if later(n):
                        dve.wait_ge(o_done, n)
                    dve.wait_ge(att_done, EC * n + c + 1)
                    dve.tensor_tensor(gated[:, c, :], p_att[:, c, :], g[p][:, c, :], ALU.mult
                                      ).then_inc(gated_ready, 1)

            def subtract_mean(t, bank):
                dve.scalar_tensor_tensor(out=o1[:, t, :], in0=bank[:, t * D:(t + 1) * D],
                                         scalar=mv2[:, t, 0:1], in1=ln2w,
                                         op0=ALU.subtract, op1=ALU.mult).then_inc(o1_ready, 1)

            def normalized(t):
                dve.scalar_tensor_tensor(out=Y[:, t, :], in0=o1[:, t, :],
                                         scalar=rstd3[:, t:t + 1], in1=rest[:, t * D:(t + 1) * D],
                                         op0=ALU.mult, op1=ALU.add).then_inc(y_ready, 1)

            def out_norm(n):
                dve.wait_ge(o_done, n + 1)
                for t in range(NT):
                    dve.bn_stats(st2[:, t, :], p_o[:, t * D:(t + 1) * D]).then_inc(stats3_ready, 1)

            def out_variances(n):
                for t in range(NT):
                    dve.bn_aggr(mv2[:, t, :], st2[:, t, :]).then_inc(aggr3_ready, 1)
                dve.wait_ge(aggr3_ready, NT * (n + 1))
                dve.tensor_scalar(var3[:], mv2[:, :, 1], EPS, None, ALU.add).then_inc(var3_ready, 1)
                for t in range(NT):
                    subtract_mean(t, p_o)

            def output(n):
                dve.wait_ge(o1_ready, NT * (n + 1))
                dve.wait_ge(rest_ready, n + 1)
                if later(n):
                    dve.wait_ge(y_stored, 16 * n)
                dve.wait_ge(rstd3_ready, n + 1)
                for t in range(NT):
                    normalized(t)

            def first():
                stats(0, 0, 0)
                dve.wait_ge(stats_ready, NT)
                variances(0)
                dve.wait_ge(rstd_xa0_ready, 1)
                norm_twice(0, 0)
                shift(0)
                dve.wait_ge(cst_loaded, 16)
                dve.wait_ge(vec_loaded, 16)
                wide_columns()
                split_weights()
                low_part(0)
                column_biases()
                position_bias()
                row_biases()
                dve.wait_ge(s_ready, 1)
                dve.tensor_tensor(Z[0:2 * QK, :, :], s[:].rearrange("p (b n) -> p b n", b=NB),
                                  rope[0:2 * QK, :].unsqueeze(1).to_broadcast([2 * QK, NB, SEQ]),
                                  ALU.mult).then_inc(Z_ready, 1)
                dve.wait_ge(w_rest_loaded, 16)
                dve.tensor_scalar(wf[:], w[:, W_F:W_F + D], 0.5, None, ALU.mult).then_inc(wf_ready, 1)

            def slot(i, p, more):
                u = i * 2 + p
                if later(u):
                    gate(1 - p, u - 1)
                if more:
                    ni, np_ = following(i, p)
                    stats(ni, np_, u + 1)
                if more:
                    dve.wait_ge(stats_ready, NT * (u + 2))
                if more and not later(u):
                    variances(u + 1)
                if later(u):
                    dve.wait_ge(r_done, u)
                dve.wait_ge(step_ready, u + 1)
                mix(xk, V_MUK)
                if more and later(u):
                    variances(u + 1)
                if later(u):
                    dve.wait_ge(row_loaded, 16)
                    out_norm(u - 1)
                    dve.wait_ge(stats3_ready, NT * u)
                mix(xr, V_MUR)
                if later(u):
                    out_variances(u - 1)
                if more:
                    shift(u + 1)
                dve.wait_ge(bias_loaded, 32)
                dve.wait_ge(scores_done, u + 1)
                dve.scalar_tensor_tensor(out=a1[:], scalar=1.0 / GROUP,
                                         in0=p_scores[:, 0:NT * GROUP].rearrange(
                                             "p (t j) -> p t j", t=NT),
                                         in1=bias[:].unsqueeze(1).to_broadcast([P, NT, GROUP]),
                                         op0=ALU.mult, op1=ALU.add).then_inc(a1_ready, 1)
                linear_keys(u)
                if later(u):
                    dve.wait_ge(att_done, EC * u)
                dve.wait_ge(a1_ready, u + 1)
                for h in range(HG):
                    at = slice(h * GROUP, (h + 1) * GROUP)
                    dve.scalar_tensor_tensor(out=a2[at, :, at], in0=a1[at, :, :], scalar=0.0,
                                             in1=a1[at, :, :], op0=ALU.max, op1=ALU.mult
                                             ).then_inc(a2_ready, 1)
                if more:
                    norm_twice(np_, u + 1)
                dve.wait_ge(heads_ready, 3 * (u + 1))
                dve.tensor_copy(lqs[2 * QK:3 * QK, :], lqs[0:QK, :].bitcast(F32)).then_inc(lq_copied, 1)
                low_kv(u)
                if more:
                    low_part(u + 1)
                if later(u):
                    output(u - 1)
                if not more:
                    gate(p, u)
                dve.wait_ge(rt_ready, u + 1)
                if later(u):
                    dve.wait_ge(rest_ready, u)
                dve.wait_ge(ffnv_done, u + 1)
                dve.scalar_tensor_tensor(out=ffn[:], in0=rt[:], scalar=1.0, in1=p_ffn,
                                         op0=ALU.add, op1=ALU.mult).then_inc(ffn_ready, 1)

            def last():
                n = units - 1
                for h in range(2):
                    half = slice(h * HT, (h + 1) * HT)
                    dve.wait_ge(o_done, n + h + 1)
                    for t in range(h * HT, (h + 1) * HT):
                        dve.bn_stats(st2[:, t, :], p_last[h][:, t * D:(t + 1) * D]
                                     ).then_inc(stats3_ready, 1)
                    dve.wait_ge(stats3_ready, NT * n + (h + 1) * HT)
                    for t in range(h * HT, (h + 1) * HT):
                        dve.bn_aggr(mv2[:, t, :], st2[:, t, :]).then_inc(aggr3_ready, 1)
                    dve.wait_ge(aggr3_ready, NT * n + (h + 1) * HT)
                    dve.tensor_scalar(var3[:, half], mv2[:, half, 1], EPS, None, ALU.add
                                      ).then_inc(var3_ready, 1)
                for t in range(NT):
                    subtract_mean(t, p_last[t // HT])
                dve.wait_ge(rest_ready, units)
                dve.wait_ge(y_stored, 16 * n)
                for t in range(NT):
                    if t % HT == 0:
                        dve.wait_ge(rstd3_ready, n + t // HT + 1)
                    dve.wait_ge(o1_ready, NT * n + t + 1)
                    normalized(t)

            pipeline(dve, first, slot, last)

        @block.scalar
        def _(act):
            act.dma_start(cst[:], consts).then_inc(cst_loaded, 16)
            act.dma_start(vec[:], vectors).then_inc(vec_loaded, 16)

            act.wait_ge(setup_pool, 1)
            act.activation(table[:], mhalf[:, 0, 0:1], ACT.Silu)
            act.dma_start(row[:], rows.unsqueeze(0).to_broadcast([P, R_ALL])).then_inc(row_loaded, 16)

            def norm(p, n):
                act.wait_ge(shift1_ready, n + 1)
                if later(n):
                    act.wait_ge(xT_done, n)
                for t in range(NT):
                    last = act.activation(xn[:, t, :], X[p][:, t, :], ACT.Identity,
                                          bias=shift1[:, t:t + 1], scale=rstd[:, 0, t:t + 1])
                last.then_inc(xn_ready, 1)

            def sigmoid(n):
                act.wait_ge(r_done, n + 1)
                if later(n):
                    act.wait_ge(ffn_ready, n)
                act.activation(rt[:], p_r, ACT.Tanh, scale=0.5).then_inc(rt_ready, 1)

            def output_bias(n, banks):
                act.wait_ge(rt_ready, n + 1)
                share = NT // len(banks)
                for h, bank in enumerate(banks):
                    act.activation(bank[:, h * share * D:(h + 1) * share * D].rearrange(
                                       "p (t d) -> p t d", t=share),
                                   row[:, R_BO:R_BO + D].unsqueeze(1).to_broadcast([P, share, D]),
                                   ACT.Identity).then_inc(obias_ready, 1)

            def high_part(n):
                if later(n):
                    act.wait_ge(v_done, 2 * n)
                act.wait_ge(xaT_done, n + 1)
                act.activation(xhi[:], p_xa, ACT.Identity).then_inc(xhi_ready, 1)

            def transposed(n, src):
                if later(n):
                    act.wait_ge(mix_ready, 2 * n)
                act.wait_ge(xT_done, n + 1)
                act.activation(xnT[:, :, 1:SEQ + 1], src.rearrange("p (b n) -> p b n", b=NB),
                               ACT.Identity).then_inc(xnT_ready, 1)

            def silu_qk(n):
                act.wait_ge(qk_done, n + 1)
                if later(n):
                    act.wait_ge(Z_ready, n)
                act.activation(s[:], p_qk[0:2 * QK, :], ACT.Silu, bias=pbias[0:2 * QK, EC:EC + 1]
                               ).then_inc(s_ready, 1)

            def silu_gate(p, n):
                for c in range(EC):
                    act.wait_ge(g_done, EC * n + c + 1)
                    if c == 0 and later(n) and later(n - 1):
                        act.wait_ge(gated_ready, EC * (n - 1))
                    act.activation(g[p][:, c, :], p_g[:, c, :], ACT.Silu, bias=pbias[:, c:c + 1]
                                   ).then_inc(g_ready, 1)

            def move_heads(n):
                act.wait_ge(heads_done, n + 1)
                if later(n):
                    act.wait_ge(att_done, EC * n)
                act.activation(hd[:], p_heads, ACT.Identity).then_inc(heads_ready, 1)
                act.activation(k[QK:2 * QK, :], p_heads[2 * QK:3 * QK, :], ACT.Identity).then_inc(heads_ready, 1)
                act.activation(lqs[0:QK, :], p_heads[0:QK, :], ACT.Identity).then_inc(heads_ready, 1)

            def value_biases(n):
                for h in range(2):
                    if later(n):
                        act.wait_ge(gated_ready, EC * (n - 1) + h + 1)
                    act.activation(p_v[:, h, :].rearrange("p (t e) -> p t e", t=2),
                                   row[:, R_BV:R_BV + E].unsqueeze(1).to_broadcast([P, 2, E]),
                                   ACT.Identity).then_inc(vbias_ready, 1)

            def silu_values(n):
                for h in range(2):
                    act.wait_ge(v_done, 2 * n + h + 1)
                    if later(n):
                        act.wait_ge(att_done, 2 * n)
                    act.activation(v[:, 2 * h:2 * h + 2, :].rearrange("p t e -> p (t e)"),
                                   p_v[:, h, :], ACT.Silu).then_inc(v_ready, 1)

            def first():
                act.wait_ge(vec_loaded, 16)
                act.wait_ge(w_loaded, 16)
                act.activation(whi[:], w[:, 0:W_O], ACT.Identity, scale=vec[:, V_LN1W:V_LN1W + 1]
                               ).then_inc(w_split, 1)
                high_part(0)
                norm(0, 0)
                act.wait_ge(pbias_ready, 1)
                silu_qk(0)
                act.wait_ge(row_ready, 1)
                value_biases(0)
                transposed(0, p_o)
                move_heads(0)
                silu_gate(0, 0)
                silu_values(0)

            def slot(i, p, more):
                u = i * 2 + p
                if more:
                    ni, np_ = following(i, p)
                    act.wait_ge(x_loaded[np_], 16 * (ni + 1))
                    norm(np_, u + 1)
                act.wait_ge(k_done, u + 1)
                if later(u):
                    act.wait_ge(kact_ready, u)
                act.activation(kr[:], p_k, ACT.Relu).then_inc(kr_ready, 1)
                if more:
                    sigmoid(u)
                act.wait_ge(kv_done, u + 1)
                if later(u):
                    act.wait_ge(att_done, EC * u)
                for b in range(NB):
                    act.activation(kvs[0:2 * QK, b, :], p_kv[2 * b * QK:2 * (b + 1) * QK, 0:E],
                                   ACT.Identity, scale=1.0 / SEQ).then_inc(kvh_ready, 1)
                if not more:
                    sigmoid(u)
                if more:
                    high_part(u + 1)
                output_bias(u, [p_o] if more else p_last)
                if more:
                    transposed(u + 1, p_xn)
                    silu_qk(u + 1)
                    silu_gate(1 - p, u + 1)
                    value_biases(u + 1)
                    move_heads(u + 1)
                    silu_values(u + 1)

            pipeline(act, first, slot)

        @block.tensor
        def _(pe):
            def warm_up():
                pe.wait_ge(idle_ready, 1)
                for i in range(WARM):
                    pe.matmul(p_v[:, i % 2, :], idle[:], idle[:].unsqueeze(1).to_broadcast([P, NT, P]),
                              start=True, stop=True)

            def setup_products():
                pe.wait_ge(posb_ready, 1)
                pe.matmul(p_posrow, posb[:], cst[0:2 * MAX_REL + 1, C_SEL:C_SEL + P],
                          start=True, stop=True).then_inc(posrow_done, 1)
                pe.wait_ge(vec_loaded, 16)
                pe.wait_ge(w_loaded, 16)
                b = vec[:, V_LN1B:V_LN1B + 1]
                for c in range(EC + 1):
                    at = W_G + c * P if c < EC else W_QK
                    pe.matmul(p_column[:, c:c + 1], w[:, at:at + P], b, start=True, stop=True)
                pe.wait_ge(ln1b_ready, 1)
                pe.matmul(p_row, ln1b_wide[:], w[:, W_V:W_V + E], start=True, stop=True
                          ).then_inc(pbias_done, 1)

            def tile(t):
                return slice(t * P, (t + 1) * P)

            def transposes_xa(n):
                if later(n):
                    pe.wait_ge(g_ready, EC * n)
                if later(n):
                    pe.wait_ge(xa_ready, NT * (n + 1))
                for t in range(NT):
                    if not later(n):
                        pe.wait_ge(xa_ready, t + 1)
                    last = pe.transpose(p_xa[:, tile(t)], xa[:, t, :], ident)
                last.then_inc(xaT_done, 1)

            def transposes_xn(n, dst):
                pe.wait_ge(xn_ready, n + 1)
                for t in range(NT):
                    last = pe.transpose(dst[:, tile(t)], xn[:, t, :], ident)
                last.then_inc(xT_done, 1)

            def project(n, dst, at):
                pe.matmul(dst, whi[:, at:at + P], xhi[:], start=True, stop=False)
                pe.matmul(dst, wlo[:, at:at + P], xhi[:], start=False, stop=False)
                pe.wait_ge(xlo_ready, n + 1)
                return pe.matmul(dst, whi[:, at:at + P], xlo[:], start=False, stop=True)

            def project_qk(n):
                pe.wait_ge(xhi_ready, n + 1)
                if later(n):
                    pe.wait_ge(kv_ready, NB * n)
                project(n, p_qk, W_QK).then_inc(qk_done, 1)

            def project_gate(n):
                if later(n):
                    pe.wait_ge(xnT_ready, n + 1)
                for c in range(EC):
                    project(n, p_g[:, c, :], W_G + c * P).then_inc(g_done, 1)

            def rotary_heads(n):
                if later(n):
                    pe.wait_ge(kr_ready, n)
                pe.wait_ge(Z_ready, n + 1)
                pe.matmul(p_heads, heads[:], Z[:].rearrange("p b n -> p (b n)"), start=True, stop=True
                          ).then_inc(heads_done, 1)

            def project_values(n):
                wv = slice(W_V, W_V + E)
                for h in range(2):
                    pe.wait_ge(vbias_ready, 2 * n + h + 1)
                    for t in range(2):
                        x = tile(2 * h + t)
                        dst = p_v[:, h, t * E:(t + 1) * E]
                        pe.matmul(dst, xhi[:, x], whi[:, wv], start=False, stop=False,
                                  skip_group_check=True)
                        pe.matmul(dst, xhi[:, x], wlo[:, wv], start=False, stop=False,
                                  skip_group_check=True)
                        last = pe.matmul(dst, xlo[:, x], whi[:, wv], start=False, stop=True,
                                         skip_group_check=True)
                    last.then_inc(v_done, 1)

            def linear_keys(n):
                for t in range(NT):
                    last = pe.transpose(p_lk[:, t * QK:(t + 1) * QK], hd[3 * QK:P, tile(t)],
                                        cst[3 * QK:P, C_ID + 3 * QK:C_ID + P])
                last.then_inc(lk_done, 1)

            def scores(u):
                if later(u):
                    pe.wait_ge(ffn_ready, u)
                pe.wait_ge(heads_ready, 3 * u + 2)
                for t in range(NT):
                    for h in range(HG):
                        x = slice(t * P + h * GROUP, t * P + (h + 1) * GROUP)
                        last = pe.matmul(p_scores[h * GROUP:(h + 1) * GROUP,
                                                  t * GROUP:(t + 1) * GROUP],
                                         k[QK:2 * QK, x], hd[QK:2 * QK, x], start=True, stop=True)
                last.then_inc(scores_done, 1)

            def mix_keys(u):
                pe.wait_ge(w_rest_loaded, 16)
                pe.wait_ge(heads_ready, 3 * (u + 1))
                pe.wait_ge(mix_ready, 2 * (u + 1))
                pe.matmul(p_k, w[:, W_K:W_K + D], xk[:].rearrange("p b n -> p (b n)"),
                          start=True, stop=True).then_inc(k_done, 1)

            def receptance(u):
                if later(u):
                    pe.wait_ge(o1_ready, NT * u)
                for t in range(NT):
                    last = pe.matmul(p_r[:, tile(t)], xr[:].rearrange("p b n -> p (b n)")[:, tile(t)],
                                     w[:, W_R:W_R + D], start=(t == 0), stop=True,
                                     skip_group_check=True)
                last.then_inc(r_done, 1)

            def keys_by_values(u):
                pe.wait_ge(v_ready, 2 * (u + 1))
                pe.wait_ge(lk_ready, u + 1)
                for t in range(2):
                    for b in range(NB):
                        for r in (2 * b, 2 * b + 1):
                            last = pe.matmul(p_kv[r * QK:(r + 1) * QK, 0:E], lk[:, 2 * b + t, :],
                                             v[:, 2 * b + t, :], start=(t == 0), stop=(t == 1))
                last.then_inc(kv_done, 1)

            def quadratic(u):
                pe.wait_ge(a2_ready, HG * (u + 1))
                for c in range(EC):
                    for t in range(NT):
                        pe.matmul(p_att[:, c, tile(t)], v[:, t, c * P:(c + 1) * P], a2[:, t, :],
                                  start=(t == 0), stop=False, skip_group_check=True)

            def linear(u):
                pe.wait_ge(lq_ready, u + 1)
                pe.wait_ge(lq_copied, u + 1)
                pe.wait_ge(kv_ready, NB * (u + 1))
                for c in range(EC):
                    for b in range(NB):
                        last = pe.matmul(p_att[:, c, b * SEQ:(b + 1) * SEQ],
                                         kvs[:, b, c * P:(c + 1) * P],
                                         lqs[:, b * SEQ:(b + 1) * SEQ],
                                         start=False, stop=True, skip_group_check=True)
                    last.then_inc(att_done, 1)

            def mix_values(u):
                pe.wait_ge(wf_ready, 1)
                pe.wait_ge(kact_ready, u + 1)
                for t in range(NT):
                    last = pe.matmul(p_ffn[:, tile(t)], kact[:, tile(t)], wf[:],
                                     start=True, stop=True)
                last.then_inc(ffnv_done, 1)

            def project_output(u, banks):
                share = NT // len(banks)
                for h, bank in enumerate(banks):
                    pe.wait_ge(obias_ready, u + h + 1)
                    pe.wait_ge(gated_ready, EC * (u + 1))
                    for t in range(h * share, (h + 1) * share):
                        for c in range(EC):
                            last = pe.matmul(bank[:, tile(t)], gated[:, c, tile(t)],
                                             w[:, W_O + c * D:W_O + (c + 1) * D], start=False,
                                             stop=(c == EC - 1), skip_group_check=True)
                    last.then_inc(o_done, 1)

            def first():
                warm_up()
                pe.wait_ge(cst_loaded, 16)
                transposes_xa(0)
                setup_products()
                pe.wait_ge(w_split, 2)
                project_qk(0)
                project_gate(0)
                transposes_xn(0, p_o)
                pe.wait_ge(heads_built, 4)
                pe.wait_ge(rope_loaded, 16)
                rotary_heads(0)
                project_values(0)

            def slot(i, p, more):
                u = i * 2 + p
                scores(u)
                linear_keys(u)
                mix_keys(u)
                if more:
                    receptance(u)
                    keys_by_values(u)
                    transposes_xa(u + 1)
                    quadratic(u)
                    mix_values(u)
                    transposes_xn(u + 1, p_xn)
                    linear(u)
                    project_qk(u + 1)
                    project_gate(u + 1)
                    project_output(u, [p_o])
                    rotary_heads(u + 1)
                    project_values(u + 1)
                else:
                    keys_by_values(u)
                    quadratic(u)
                    linear(u)
                    receptance(u)
                    mix_values(u)
                    project_output(u, p_last)

            pipeline(pe, first, slot)


def constants():
    import numpy as np
    half = QK // 2
    c = np.zeros((P, C_ALL), np.float32)
    c[:, C_ID:C_ID + P] = np.eye(P)
    inv = np.float32(10000.0) ** (-np.arange(half, dtype=np.float32) / np.float32(half))
    angle = np.arange(SEQ, dtype=np.float32)[None, :] * inv.astype(np.float32)[:, None]
    cos, sin = np.cos(angle.astype(np.float64)), np.sin(angle.astype(np.float64))
    table = np.concatenate([cos, cos, -sin, sin])
    c[:, C_ROPE:C_ROPE + SEQ] = np.concatenate([table, table])
    c[:, C_HEADEYE:C_HEADEYE + QK] = np.tile(np.eye(QK), (4, 1))
    away = np.minimum(np.abs(np.arange(P) - (GROUP - 1)), MAX_REL)
    c[:, C_SEL:C_SEL + P] = np.arange(P)[:, None] == away[None, :]
    return c


def kernel(L0_attn_x, L0_attn_ln1_w, L0_attn_ln1_b, L0_attn_Wqk, L0_attn_bqk, L0_attn_Wv, L0_attn_bv,
           L0_attn_Wg, L0_attn_bg, L0_attn_Wo, L0_attn_bo, L0_attn_ln2_w, L0_attn_ln2_b, L0_attn_gamma,
           L0_attn_beta, L0_attn_pos_emb, L0_ffn_W_r, L0_ffn_W_k, L0_ffn_W_v, L0_ffn_mu_r, L0_ffn_mu_k):
    import numpy as np
    import concourse.bacc as bacc
    from concourse.bass_utils import run_bass_kernel_spmd

    x = np.ascontiguousarray(L0_attn_x)
    half = QK // 2
    swap = np.r_[half:QK, 0:half]
    wo = np.asarray(L0_attn_Wo).T
    weights = np.concatenate(
        [L0_attn_Wqk.T, np.asarray(L0_attn_Wqk)[swap].T, L0_attn_Wv.T, L0_attn_Wg.T, wo[:P], wo[P:],
         L0_ffn_W_r.T, L0_ffn_W_k.T, L0_ffn_W_v.T], axis=1)
    vectors = np.zeros((P, V_ALL), np.float32)
    vectors[:, V_LN1W] = L0_attn_ln1_w
    vectors[:, V_LN1B] = L0_attn_ln1_b
    vectors[:, V_MUR] = L0_ffn_mu_r
    vectors[:, V_MUK] = L0_ffn_mu_k
    vectors[:, V_BG:V_BG + EC] = np.asarray(L0_attn_bg).reshape(EC, P).T
    bqk, gamma, beta = np.asarray(L0_attn_bqk), np.asarray(L0_attn_gamma), np.asarray(L0_attn_beta)
    vectors[0:2 * QK, V_BQK] = np.concatenate([bqk, bqk[swap]])
    heads = np.concatenate([gamma.T, gamma.T[swap], beta.T, beta.T[swap]])
    vectors[:, V_HEADS:V_HEADS + 4] = heads[:, [1, 0, 2, 3]]
    vectors[0:2 * MAX_REL + 1, V_POS] = L0_attn_pos_emb

    ins = {
        "x": x, "weights": np.ascontiguousarray(weights), "vectors": vectors,
        "rows": np.concatenate([L0_attn_bv, L0_attn_bo, L0_attn_ln2_w, L0_attn_ln2_b]), "consts": constants(),
    }
    nc = bacc.Bacc("TRN2", target_bir_lowering=False, num_devices=1)
    args = {name: nc.dram_tensor(f"in_{name}", a.shape, mybir.dt.from_np(a.dtype),
                                 kind="ExternalInput").ap() for name, a in ins.items()}
    out = nc.dram_tensor("out_y", x.shape, F32, kind="ExternalOutput").ap()
    block_kernel(nc, out=out, **args)
    r = run_bass_kernel_spmd(nc, [{f"in_{name}": a for name, a in ins.items()}], core_ids=[0])
    return r.results[0]["out_y"]
```
